# Optimizing a Trainium2 kernel written in Bass

```python
import numpy as np
import jax
import jax.numpy as jnp

def _softmax(x, axis=-1):
    return jax.nn.softmax(x, axis=axis)

def _gelu(x):
    return jax.nn.gelu(x, approximate=True)

def _silu(x):
    return jax.nn.silu(x)

def _sigmoid(x):
    return jax.nn.sigmoid(x)

def _layernorm(x, axis=-1, eps=1e-05):
    m = jnp.mean(x, axis=axis, keepdims=True)
    v = jnp.var(x, axis=axis, keepdims=True)
    return (x - m) / jnp.sqrt(v + eps)

def _scatter_add(tgt, idx, src, axis=0):
    return tgt.at[idx].add(src)

def _segment_sum(src, seg, n):
    return jax.ops.segment_sum(src, seg, n)
kernel_name = 'mk_prb_d1_jaxref_r8_41c45a'

def setup_inputs(seed: int=0):
    np.random.seed(seed)
    _w = jnp.asarray

    def _L0_attn_setup():
        import jax, jax.numpy as jnp
        import numpy as np
        D_MODEL = 128
        NUM_HEADS = 16
        HEAD_DIM = D_MODEL // NUM_HEADS
        BATCH = 64
        SEQ = 64

        def _rope(x):
            B, S, D = x.shape
            half = D // 2
            inv_freq = 1.0 / 10000.0 ** (jnp.arange(half, dtype=jnp.float32) / half)
            ang = jnp.arange(S, dtype=jnp.float32)[:, None] * inv_freq[None, :]
            cos, sin = (jnp.cos(ang), jnp.sin(ang))
            xe, xo = (x[..., 0::2], x[..., 1::2])
            out_e = xe * cos - xo * sin
            out_o = xe * sin + xo * cos
            return jnp.stack([out_e, out_o], axis=-1).reshape(B, S, D)
        key = jax.random.key(seed)
        ks = jax.random.split(key, 9)
        s = 1.0 / np.sqrt(D_MODEL)
        return {'x': jax.random.normal(ks[0], (BATCH, SEQ, D_MODEL), dtype=jnp.float32), 'Wq': jax.random.normal(ks[1], (D_MODEL, D_MODEL), dtype=jnp.float32) * s, 'bq': jax.random.normal(ks[2], (D_MODEL,), dtype=jnp.float32) * s, 'Wk': jax.random.normal(ks[3], (D_MODEL, D_MODEL), dtype=jnp.float32) * s, 'bk': jax.random.normal(ks[4], (D_MODEL,), dtype=jnp.float32) * s, 'Wv': jax.random.normal(ks[5], (D_MODEL, D_MODEL), dtype=jnp.float32) * s, 'bv': jax.random.normal(ks[6], (D_MODEL,), dtype=jnp.float32) * s, 'Wo': jax.random.normal(ks[7], (D_MODEL, D_MODEL), dtype=jnp.float32) * s, 'bo': jax.random.normal(ks[8], (D_MODEL,), dtype=jnp.float32) * s}
    _L0_attn_in = _L0_attn_setup()

    def _L0_ffn_setup():
        import jax, jax.numpy as jnp
        import numpy as np
        FP8_MAX = 448.0

        def quant_fp8(x):
            amax = jnp.max(jnp.abs(x)).astype(jnp.float32)
            scale = jnp.minimum(FP8_MAX / jnp.maximum(amax, 1e-12), FP8_MAX)
            x_fp8 = jnp.clip(x * scale, -FP8_MAX, FP8_MAX).astype(jnp.float8_e4m3fn)
            return (x_fp8, 1.0 / scale)
        key = jax.random.key(seed)
        k1, k2, k3 = jax.random.split(key, 3)
        B, S, IN, OUT = (4, 1024, 128, 128)
        input = jax.random.normal(k1, (B, S, IN), dtype=jnp.float32)
        bound = 1.0 / np.sqrt(IN)
        weight = jax.random.uniform(k2, (OUT, IN), dtype=jnp.float32, minval=-bound, maxval=bound)
        bias = jax.random.uniform(k3, (OUT,), dtype=jnp.float32, minval=-bound, maxval=bound)
        return {'input': input, 'weight': weight, 'bias': bias}
    _L0_ffn_in = _L0_ffn_setup()
    _d = {'L0_attn_x': _L0_attn_in['x'], 'L0_attn_Wq': _L0_attn_in['Wq'], 'L0_attn_bq': _L0_attn_in['bq'], 'L0_attn_Wk': _L0_attn_in['Wk'], 'L0_attn_bk': _L0_attn_in['bk'], 'L0_attn_Wv': _L0_attn_in['Wv'], 'L0_attn_bv': _L0_attn_in['bv'], 'L0_attn_Wo': _L0_attn_in['Wo'], 'L0_attn_bo': _L0_attn_in['bo'], 'L0_ffn_weight': _L0_ffn_in['weight'], 'L0_ffn_bias': _L0_ffn_in['bias']}
    _x0 = _d['L0_attn_x']
    _d['L0_attn_x'] = jax.random.normal(jax.random.fold_in(jax.random.key(seed), 1), (32, 256, 128), dtype=_x0.dtype)
    del _x0
    return _d

def reference(L0_attn_x, L0_attn_Wq, L0_attn_bq, L0_attn_Wk, L0_attn_bk, L0_attn_Wv, L0_attn_bv, L0_attn_Wo, L0_attn_bo, L0_ffn_weight, L0_ffn_bias):

    def _L0_attn_ref(x, Wq, bq, Wk, bk, Wv, bv, Wo, bo):
        import jax, jax.numpy as jnp
        import numpy as np
        D_MODEL = 128
        NUM_HEADS = 16
        HEAD_DIM = D_MODEL // NUM_HEADS
        BATCH = 64
        SEQ = 64

        def _rope(x):
            B, S, D = x.shape
            half = D // 2
            inv_freq = 1.0 / 10000.0 ** (jnp.arange(half, dtype=jnp.float32) / half)
            ang = jnp.arange(S, dtype=jnp.float32)[:, None] * inv_freq[None, :]
            cos, sin = (jnp.cos(ang), jnp.sin(ang))
            xe, xo = (x[..., 0::2], x[..., 1::2])
            out_e = xe * cos - xo * sin
            out_o = xe * sin + xo * cos
            return jnp.stack([out_e, out_o], axis=-1).reshape(B, S, D)
        B, S, D = x.shape
        q = _rope(x @ Wq.T + bq)
        k = _rope(x @ Wk.T + bk)
        v = x @ Wv.T + bv
        q = q.reshape(B, S, NUM_HEADS, HEAD_DIM).transpose(0, 2, 1, 3)
        k = k.reshape(B, S, NUM_HEADS, HEAD_DIM).transpose(0, 2, 1, 3)
        v = v.reshape(B, S, NUM_HEADS, HEAD_DIM).transpose(0, 2, 1, 3)
        scale = 1.0 / np.sqrt(HEAD_DIM)
        scores = jnp.einsum('bhqd,bhkd->bhqk', q, k) * scale
        attn = jax.nn.softmax(scores, axis=-1)
        vals = jnp.einsum('bhqk,bhkd->bhqd', attn, v)
        vals = vals.transpose(0, 2, 1, 3).reshape(B, S, D)
        return vals @ Wo.T + bo

    def _L0_ffn_ref(input, weight, bias):
        import jax, jax.numpy as jnp
        import numpy as np
        FP8_MAX = 448.0

        def quant_fp8(x):
            amax = jnp.max(jnp.abs(x)).astype(jnp.float32)
            scale = jnp.minimum(FP8_MAX / jnp.maximum(amax, 1e-12), FP8_MAX)
            x_fp8 = jnp.clip(x * scale, -FP8_MAX, FP8_MAX).astype(jnp.float8_e4m3fn)
            return (x_fp8, 1.0 / scale)
        prev_shape = input.shape
        x2d = input.reshape(-1, weight.shape[1])
        w_fp8, w_scale = quant_fp8(weight)
        x_fp8, x_scale = quant_fp8(x2d)
        acc = jnp.matmul(x_fp8.astype(jnp.float32), w_fp8.astype(jnp.float32).T)
        out2d = (acc * (x_scale * w_scale) + bias).astype(jnp.bfloat16)
        out = out2d.reshape(*prev_shape[:-1], weight.shape[0]).astype(input.dtype)
        return out
    x = L0_attn_x
    xn = _layernorm(x, axis=-1)
    x = x + _L0_attn_ref(xn, L0_attn_Wq, L0_attn_bq, L0_attn_Wk, L0_attn_bk, L0_attn_Wv, L0_attn_bv, L0_attn_Wo, L0_attn_bo) + _L0_ffn_ref(xn, L0_ffn_weight, L0_ffn_bias)
    return x

_drawn_inputs = setup_inputs


def setup_inputs(seed=0):
    import zlib

    import numpy as np

    out = dict(_drawn_inputs(seed))
    spreads = {}
    factors = {'L0_attn_bq': 6.245, 'L0_attn_bk': 8.0}
    for name, (base, spread) in spreads.items():
        noise = np.random.default_rng([zlib.crc32(name.encode()), seed]).standard_normal(out[name].shape)
        drawn = base * np.exp(spread * noise) if base else spread * noise
        out[name] = jnp.asarray(drawn.astype(out[name].dtype))
    for name, factor in factors.items():
        out[name] = (out[name] * factor).astype(out[name].dtype)
    return out
```

```python
from contextlib import ExitStack

import concourse.bass as bass
from concourse import mybir

ALU = mybir.AluOpType
ACT = mybir.ActivationFunctionType
AX = mybir.AxisListType
F32 = mybir.dt.float32
F16 = mybir.dt.float16
BF16 = mybir.dt.bfloat16
I32 = mybir.dt.int32

P = 128
BATCH, SEQ, HEADS = 32, 256, 16
HEAD = P // HEADS
TILES = BATCH * SEQ // P
QUADS = HEADS // 4
SCALE = HEAD ** -0.5
EPS = 1e-5
FP8_MAX = 448.0
MAGIC = 1.5 * 2.0 ** 20
TINY = 2.0 ** -6
EXPONENT = 0x7F800000
LEAD = 5
UNROLL = 4
ROUNDS = BATCH // UNROLL
GROUP = 8
GROUPS = TILES // GROUP
T_ID, T_COS, T_SIN, T_FLAG = 0, P, P + SEQ, P + 2 * SEQ
T_COLS = T_FLAG + 1

EVEN = {1: ("out", -2), 2: ("q", 4), 3: ("q_swapped", 4), 4: ("turn_maxima", 1), 5: ("turn_values", -1),
        6: ("k", 4), 7: ("turn_heads", -1)}
ODD = {0: ("k_swapped", 3), 1: ("out", -2), 2: ("v", 1), 4: ("turn_maxima", 1), 5: ("turn_values", -1),
       7: ("turn_heads", -1)}

LATER_GROUPS = {(-4, 0): 1, (-4, 2): 2, (-4, 4): 3, (-4, 6): 4, (-3, 0): 5, (-3, 2): 6, (-3, 4): 7}


def plan_side_jobs():
    at = {}
    for n in range(-4, BATCH + 2):
        for s in range(8):
            name, ahead = (ODD if n % 2 else EVEN).get(s, (None, 0))
            if name and 0 <= n + ahead < BATCH:
                at[name, n + ahead] = len(at)
    return at


def attention_and_ffn(nc, tables, x, wq, bq, wk, bk, wv, bv, wo, bo, wf, bf, out):
    side_at = plan_side_jobs()
    per_round = len(EVEN) * 2 + len(ODD) * 2

    def exists(it, k):
        return not isinstance(it, int) or 0 <= UNROLL * it + k < BATCH

    def batch(it, k):
        return it * UNROLL + k

    def lead_in(it):
        return isinstance(it, int) and it < 0

    def later_group(it, k, s):
        return LATER_GROUPS.get((UNROLL * it + k, s)) if lead_in(it) else None

    def side(name, it, k):
        if isinstance(it, int):
            return side_at.get((name, UNROLL * it + k), -1) + 1
        first = side_at[name, UNROLL + k]
        for r in range(1, ROUNDS - 1):
            assert side_at[name, UNROLL * r + k] == first + per_round * (r - 1)
        return it * per_round + (first - per_round + 1)

    def due(count):
        return not isinstance(count, int) or count > 0

    def pass_wait(engine, semaphore):
        engine.sem_inc(semaphore, 1)

    def rounds(engine, body):
        body(-1)
        body(0)
        with engine.Fori(1, ROUNDS - 1) as it:
            body(it)
        body(ROUNDS - 1)

    with ExitStack() as ctx:
        def sbuf(name, shape, dt):
            return ctx.enter_context(nc.sbuf_tensor(name, shape, dt))

        def psum(name, shape, dt):
            return ctx.enter_context(nc.psum_tensor(name, shape, dt))

        def sem(name):
            return ctx.enter_context(nc.semaphore(name))

        scratch = [[nc.dram_tensor(f"scratch_{n}{r}", [P, 4, 2 * SEQ], F16, kind="Internal").ap()
                    for r in range(2)] for n in "qk"]

        table = sbuf("table", [P, T_COLS], F32)
        ident = table[:, T_ID:T_ID + P]
        cos, sin = table[:, T_COS:T_COS + SEQ], table[:, T_SIN:T_SIN + SEQ]
        ident16 = sbuf("ident16", [P, P], F16)
        identb = sbuf("identb", [P, P], BF16)
        raw = sbuf("raw", [P, 5, P], F32)
        wo_order = sbuf("wo_order", [P, P], F32)
        wqT = sbuf("wqT", [P, 2, P], F32)
        wkT = sbuf("wkT", [P, 2, P], F32)
        wvT = sbuf("wvT", [P, P], F32)
        woT = sbuf("woT", [P, P], F32)
        w8 = sbuf("w8", [P, P], BF16)
        w8T = sbuf("w8T", [P, P], BF16)
        bias_rows = sbuf("bias_rows", [3, 3, P], F32)
        bias_cols = sbuf("bias_cols", [P, 3, 3], F32)
        bv_wide = sbuf("bv_wide", [P, P], F32)
        bo_rows = sbuf("bo_rows", [P, P], F32)
        bf_rows = sbuf("bf_rows", [P, P], F32)
        small = sbuf("small", [P, 16], F32)
        quant_w = sbuf("quant_w", [P, 4, P], F32)
        fill = sbuf("fill", [P, 2, 2 * SEQ], F16)

        xg = sbuf("xg", [P, 2, GROUP, P], F32)
        xn = sbuf("xn", [P, 2, GROUP, P], F32)
        stats = sbuf("stats", [P, GROUP, 6], F32)
        moments = sbuf("moments", [P, 2, GROUP, 2], F32)
        spread = sbuf("spread", [P, 2, GROUP], F32)
        root = sbuf("root", [P, 2, GROUP], F32)
        rstd = sbuf("rstd", [P, 2, GROUP], F32)
        newton = sbuf("newton", [P, GROUP], F32)
        largest = sbuf("largest", [P, GROUPS], F32)
        xnT = sbuf("xnT", [P, BATCH * SEQ], F32)

        xc = sbuf("xc", [P, 2, 2 * SEQ], F32)
        turned = sbuf("turned", [P, 2, 2, 2 * SEQ], F32)
        rotated = sbuf("rotated", [P, 2 * SEQ], F32)
        parts = sbuf("parts", [P, 2, 2, 2 * SEQ], F16)
        q_stack = sbuf("q_stack", [P, UNROLL, QUADS, SEQ], F16)
        k_stack = sbuf("k_stack", [P, UNROLL, HEADS, SEQ], F16)
        maxima = sbuf("maxima", [P, 2, 2, HEADS], F16)
        max_rows = sbuf("max_rows", [HEADS, 2, SEQ], F16)
        probs = sbuf("probs", [P, 8, 2 * SEQ], F32)
        v_pad = sbuf("v_pad", [P, UNROLL, 2, HEADS, 32], F32)
        valuesT = sbuf("valuesT", [P, 2 * SEQ], F32)
        inverse = sbuf("inverse", [P, 32], F32)
        heads = sbuf("heads", [P, SEQ], F32)
        headsT = sbuf("headsT", [P, SEQ], F32)
        x8_scaled = sbuf("x8_scaled", [P, SEQ], F32)
        x8_clipped = sbuf("x8_clipped", [P, SEQ], F32)
        x8_magic = sbuf("x8_magic", [P, 2, SEQ], F32)
        x8_sum = sbuf("x8_sum", [P, SEQ], F32)
        x8 = sbuf("x8", [P, 2, SEQ], BF16)
        x_rows = sbuf("x_rows", [P, 2, 2, P], F32)
        x_bias = sbuf("x_bias", [P, 2, P], F32)
        ffn = sbuf("ffn", [P, 2, P], BF16)
        attn = sbuf("attn", [P, 2, P], F32)
        result = sbuf("result", [P, 2, 2, P], F32)

        ps_rows = [psum(f"ps_rows{r}", [P, 4, SEQ], F32) for r in range(2)]
        ps_cols = [psum(f"ps_cols{r}", [P, 2 * SEQ], F32) for r in range(2)]
        ps_values = psum("ps_values", [P, 2 * SEQ], F32)
        ps_side = psum("ps_side", [P, 2 * SEQ], F32)
        ps_side16 = ps_side[:].bitcast(F16)
        ps_sideb = ps_side[:].bitcast(BF16)

        setup_loaded = sem("setup_loaded")
        dve_step = sem("dve_step")
        pool_filled = sem("pool_filled")
        biases_turned = sem("biases_turned")
        weights_turned = sem("weights_turned")
        weights_ready = sem("weights_ready")
        fill_stored = sem("fill_stored")
        weight_reduced = sem("weight_reduced")
        weight_quantised = sem("weight_quantised")
        weight8_turned = sem("weight8_turned")
        bias_summed = sem("bias_summed")
        rows_loaded = [sem(f"rows_loaded{r}") for r in range(2)]
        variance_ready = sem("variance_ready")
        root_ready = sem("root_ready")
        rstd_ready = sem("rstd_ready")
        normalised = sem("normalised")
        group_largest = sem("group_largest")
        group_turned = sem("group_turned")
        group_copied = sem("group_copied")
        largest_ready = sem("largest_ready")
        largest_reduced = sem("largest_reduced")
        scales_ready = sem("scales_ready")

        sp_passed, pool_passed, dve_passed = sem("sp_passed"), sem("pool_passed"), sem("dve_passed")

        xc_loaded = [sem(f"xc_loaded{r}") for r in range(2)]
        side_written = sem("side_written")
        side_read = sem("side_read")
        pool_rotated = sem("pool_rotated")
        high_cut = sem("high_cut")
        low_cut = sem("low_cut")
        parts_stored = [sem(f"parts_stored{c}") for c in "qk"]
        stack_loaded = [sem(f"stack_loaded{r}") for r in range(UNROLL)]
        shift_loaded = [sem(f"shift_loaded{r}") for r in range(UNROLL)]
        rows_scored = sem("rows_scored")
        rows_reduced = sem("rows_reduced")
        cols_scored = sem("cols_scored")
        probs_ready = sem("probs_ready")
        values_summed = sem("values_summed")
        values_copied = sem("values_copied")
        sums_inverted = sem("sums_inverted")
        x8_scaled_ready = sem("x8_scaled_ready")
        x8_exponent_ready = sem("x8_exponent_ready")
        x8_clipped_ready = sem("x8_clipped_ready")
        x8_magic_ready = sem("x8_magic_ready")
        x8_sum_ready = sem("x8_sum_ready")
        x8_ready = sem("x8_ready")
        x_loaded = [sem(f"x_loaded{r}") for r in range(2)]
        x_bias_ready = sem("x_bias_ready")
        result_ready = sem("result_ready")
        stored = [sem(f"stored{r}") for r in range(2)]

        amax_w, amax_w_all, scale_w, inv_w = (small[:, i:i + 1] for i in range(4))
        amax_x, amax_x_all, scale_x, inv_x = (small[:, i:i + 1] for i in range(4, 8))
        unscale = small[:, 8:9]
        SETUP_LOADS = 11

        def swapped(ap):
            return ap.rearrange("p (i two) -> p i two", two=2)

        block = ctx.enter_context(nc.Block())

        @block.sync
        def _(sp):
            sp.dma_start(table[:], tables).then_inc(setup_loaded, 16)
            for i, w in enumerate((wq, wk, wv, wo, wf)):
                sp.dma_start(raw[:, i, :], w).then_inc(setup_loaded, 16)
            for i, b in enumerate((bq, bk, bv)):
                sp.dma_start(bias_rows[i:i + 1, 0, :], b.rearrange("(one f) -> one f", one=1)).then_inc(setup_loaded, 16)
            sp.dma_start(bo_rows[:], bo.partition_broadcast(P)).then_inc(setup_loaded, 16)
            sp.dma_start(bf_rows[:], bf.partition_broadcast(P)).then_inc(setup_loaded, 16)

            sp.wait_ge(pool_filled, 3)
            for c in range(2):
                for r in range(2):
                    sp.dma_start(scratch[c][r][:, 3, :], fill[:, c, :]).then_inc(fill_stored, 16)
            sp.wait_ge(fill_stored, 64)

            def load_xc(it, k):
                if exists(it, k):
                    r = (k // 2) % 2
                    sp.wait_ge(group_copied, it + k // 4 + 1)
                    pass_wait(sp, sp_passed)
                    if due(count := side("v", it, k - 4)):
                        sp.wait_ge(side_written, count)
                        pass_wait(sp, sp_passed)
                    src = xnT[:, bass.ds(batch(it, k) * SEQ, 2 * SEQ)]
                    sp.dma_start(xc[:, r, :], src).then_inc(xc_loaded[r], 16)

            def store_parts(c, it, k):
                if not exists(it, k):
                    return
                r = (k // 2) % 2
                pair = it * 2 + k // 2
                for b in range(2):
                    if due(count := (it + (k - 4) // 4 + 1) * 80):
                        sp.wait_ge(stack_loaded[(k + b) % UNROLL], count)
                        pass_wait(sp, sp_passed)
                sp.wait_ge(low_cut, pair * 2 + c + 1)
                pass_wait(sp, sp_passed)
                one, two = (slice(0, 1), slice(1, 3)) if c == 0 else (slice(2, 3), slice(0, 2))
                sp.dma_start(scratch[c][r][:, one, :], parts[:, c, 0:1, :]).then_inc(parts_stored[c], 16)
                sp.dma_start(scratch[c][r][:, two, :], parts[:, c, :, :]).then_inc(parts_stored[c], 16)

            def load_stacks(it, k):
                if not exists(it, k):
                    return
                r, b, buf = (k // 2) % 2, k % 2, k % UNROLL
                pair = it * 2 + k // 2
                cols = slice(b * SEQ, (b + 1) * SEQ)
                if due(count := (batch(it, k) - 3) * HEADS):
                    sp.wait_ge(cols_scored, count)
                    pass_wait(sp, sp_passed)
                sp.wait_ge(parts_stored[0], pair * 32 + 32)
                pass_wait(sp, sp_passed)
                src = scratch[0][r].rearrange("(t f) c w -> (f c) t w", t=QUADS)
                sp.dma_start(q_stack[:, buf], src[:, :, cols]).then_inc(stack_loaded[buf], 16)
                sp.wait_ge(parts_stored[1], pair * 32 + 32)
                pass_wait(sp, sp_passed)
                src = scratch[1][r].rearrange("(t f) c w -> (f c) t w", t=QUADS)
                for j in range(4):
                    rows = slice(32 * j, 32 * j + 32)
                    sp.dma_start(k_stack[rows, buf, j:HEADS:4, :], src[rows, :, cols])\
                      .then_inc(stack_loaded[buf], 16)

            def load_shift(it, k):
                if not exists(it, k):
                    return
                buf = k % UNROLL
                sp.wait_ge(side_read, side("turn_maxima", it, k))
                pass_wait(sp, sp_passed)
                for t in range(QUADS):
                    sp.dma_start(q_stack[3:P:32, buf, t, :], max_rows[4 * t:4 * t + 4, k % 2, :])\
                      .then_inc(shift_loaded[buf], 16)

            def store_result(it, k):
                if exists(it, k):
                    sp.wait_ge(result_ready, batch(it, k) + 1)
                    pass_wait(sp, sp_passed)
                    dst = out[bass.ds(batch(it, k), 1)].rearrange("o (t p) d -> p (o t) d", p=P)
                    sp.dma_start(dst, result[:, k % 2]).then_inc(stored[k % 2], 16)

            def load_x(it, k):
                if exists(it, k):
                    if due(count := batch(it, k) - 1):
                        sp.wait_ge(x_bias_ready, count)
                        pass_wait(sp, sp_passed)
                    src = x[bass.ds(batch(it, k), 1)].rearrange("o (t p) d -> p (o t) d", p=P)
                    sp.dma_start(x_rows[:, k % 2], src).then_inc(x_loaded[k % 2], 16)

            def body(it):
                for k in range(0, UNROLL, 2):
                    load_xc(it, k + 4)
                    store_result(it, k - 3)
                    load_stacks(it, k + 3)
                    load_shift(it, k + 1)
                    load_x(it, k)
                    store_parts(0, it, k + 4)
                    store_parts(1, it, k + 4)
                    store_result(it, k - 2)
                    load_x(it, k + 1)
                    load_shift(it, k + 2)
                    load_stacks(it, k + 4)

            rounds(sp, body)
            for k in (-3, -2, -1):
                store_result(ROUNDS, k)
            for r in range(2):
                sp.wait_ge(stored[r], BATCH // 2 * 16)

        @block.gpsimd
        def _(pool):
            g = nc.gpsimd
            g.memset(k_stack[:], 0.0).then_inc(pool_filled, 1)
            g.memset(v_pad[:], 0.0).then_inc(pool_filled, 1)
            pool.wait_ge(setup_loaded, 16 * SETUP_LOADS)
            g.memset(fill[:, 0, :], 0.0)
            g.tensor_scalar(fill[:, 1, :], table[:, T_FLAG:T_FLAG + 1].to_broadcast([P, 2 * SEQ]), 1.0, None,
                            ALU.mult).then_inc(pool_filled, 1)
            pool.wait_ge(pool_filled, 3)
            quads = v_pad[:].rearrange("p b kt (g e j) c -> p (b kt g) e j c", e=2, j=4)
            for e in range(2):
                g.memset(quads[:, :, e, :, 16 * e + 8], 1.0).then_inc(pool_filled, 1)

            pool.wait_ge(dve_step, 1)
            g.partition_all_reduce(amax_w_all, amax_w, P, bass.bass_isa.ReduceOp.absmax).then_inc(weight_reduced, 1)

            def cut(c, it, k):
                if not exists(it, k):
                    return
                done = (it * 2 + k // 2) * 2 + c
                pool.wait_ge(side_read, side(("q_swapped", "k_swapped")[c], it, k))
                if due(count := done):
                    pool.wait_ge(low_cut, count)
                g.tensor_tensor(rotated[:], turned[:, c, 0, :], turned[:, c, 1, :], ALU.add).then_inc(pool_rotated, 1)
                pool.wait_ge(pool_rotated, done + 1)
                if due(count := (it * 2 + k // 2) * 32):
                    pool.wait_ge(parts_stored[c], count)
                pass_wait(pool, pool_passed)
                g.tensor_scalar(parts[:, c, 0, :], rotated[:], 1.0, None, ALU.mult).then_inc(high_cut, 1)
                pool.wait_ge(high_cut, done + 1)
                g.tensor_tensor(parts[:, c, 1, :], rotated[:], parts[:, c, 0, :], ALU.subtract).then_inc(low_cut, 1)

            def add_bias(it, k):
                if exists(it, k):
                    pool.wait_ge(x_loaded[k % 2], (it * 2 + k // 2 + 1) * 16)
                    if due(count := side("out", it, k - 1)):
                        pool.wait_ge(side_read, count)
                    bias = bo_rows[:].rearrange("p (one d) -> p one d", one=1).to_broadcast([P, 2, P])
                    g.tensor_tensor(x_bias[:], x_rows[:, k % 2], bias, ALU.add).then_inc(x_bias_ready, 1)

            def quantise(it, k):
                if not exists(it, k):
                    return
                n = batch(it, k) + 1
                if due(count := n - 1):
                    pool.wait_ge(x8_ready, count)
                pool.wait_ge(x8_exponent_ready, n)
                pass_wait(pool, pool_passed)
                g.tensor_scalar(x8_magic[:, 1, :], x8_magic[:, 0, :], TINY, MAGIC, ALU.max, ALU.mult)\
                 .then_inc(x8_magic_ready, 1)
                g.tensor_scalar(x8_clipped[:], x8_scaled[:], -FP8_MAX, None, ALU.max).then_inc(x8_clipped_ready, 1)
                pool.wait_ge(x8_magic_ready, n)
                pool.wait_ge(x8_clipped_ready, n)
                g.tensor_tensor(x8_sum[:], x8_clipped[:], x8_magic[:, 1, :], ALU.add).then_inc(x8_sum_ready, 1)
                pool.wait_ge(x8_sum_ready, n)
                if due(count := side("out", it, k - 2)):
                    pool.wait_ge(side_written, count)
                g.tensor_tensor(x8[:, k % 2, :], x8_sum[:], x8_magic[:, 1, :], ALU.subtract).then_inc(x8_ready, 1)

            def finish(it, k):
                if exists(it, k):
                    pool.wait_ge(side_read, side("out", it, k))
                    if due(count := (it * 2 + k // 2) * 16):
                        pool.wait_ge(stored[k % 2], count)
                    g.tensor_tensor(result[:, k % 2], attn[:], ffn[:], ALU.add).then_inc(result_ready, 1)

            def body(it):
                for k in range(UNROLL):
                    if lead_in(it) and k == 2:
                        pool.wait_ge(largest_ready, 1)
                        g.partition_all_reduce(amax_x_all, amax_x, P, bass.bass_isa.ReduceOp.absmax)\
                         .then_inc(largest_reduced, 1)
                    if k % 2:
                        cut(1, it, k + 3)
                    finish(it, k - 2)
                    add_bias(it, k - 1)
                    if k % 2 == 0:
                        cut(0, it, k + 4)
                    quantise(it, k)

            rounds(pool, body)
            finish(ROUNDS, -2)
            add_bias(ROUNDS, -1)
            finish(ROUNDS, -1)

        @block.scalar
        def _(act):
            x_tiles = x.rearrange("b (t p) d -> (b t) p d", p=P)

            def load_group(group):
                if due(count := group - 1):
                    act.wait_ge(normalised, count)
                act.dma_start(xg[:, group % 2], x_tiles[group * GROUP:(group + 1) * GROUP].rearrange("t p d -> p t d"))\
                   .then_inc(rows_loaded[group % 2], 16)

            def take_root(group):
                r = group % 2
                act.wait_ge(variance_ready, group + 1)
                nc.scalar.activation(root[:, r, :], spread[:, r, :], ACT.Sqrt).then_inc(root_ready, 1)

            def copy_group(group):
                r = group % 2
                act.wait_ge(group_turned, group + 1)
                nc.scalar.copy(xnT[:, group * GROUP * P:(group + 1) * GROUP * P],
                               ps_rows[r][:].rearrange("p a b -> p (a b)")).then_inc(group_copied, 1)

            load_group(0)
            load_group(1)
            take_root(0)
            copy_group(0)

            def exponentials(it, k, s):
                if not exists(it, k):
                    return
                for h in (2 * s, 2 * s + 1):
                    done = batch(it, k) * HEADS + h
                    if h % 4 == 0:
                        if due(count := batch(it, k) * QUADS + h // 4 - 1):
                            act.wait_ge(values_summed, count)
                    act.wait_ge(cols_scored, done + 1)
                    nc.scalar.activation(probs[:, h % 8, :], ps_cols[h % 2][:], ACT.Exp, scale=SCALE)\
                      .then_inc(probs_ready, 1)

            def side_job(it, k, s):
                name, ahead = (ODD if k % 2 else EVEN).get(s, (None, 0))
                j = k + ahead
                if name not in ("v", "turn_maxima", "turn_heads") or not exists(it, j):
                    return
                act.wait_ge(side_written, side(name, it, j))
                if name == "turn_maxima":
                    if due(count := (it + (j - 2) // 4 + 1) * 64):
                        act.wait_ge(shift_loaded[(j - 2) % UNROLL], count)
                    ins = nc.scalar.copy(max_rows[:, j % 2, :], ps_side16[0:HEADS, 0:SEQ])
                elif name == "turn_heads":
                    if due(count := side("out", it, j - 1)):
                        act.wait_ge(side_written, count)
                    ins = nc.scalar.copy(headsT[:], ps_side[:, 0:SEQ])
                else:
                    if due(count := (batch(it, j) - 2) * QUADS):
                        act.wait_ge(values_summed, count)
                    act.wait_ge(pool_filled, 5)
                    for b in range(2):
                        src = ps_side[:, b * SEQ:(b + 1) * SEQ].rearrange("p (a e j d) -> p a e j d", e=2, j=4, d=HEAD)
                        dst = v_pad[:, (j + b) % UNROLL].rearrange("p kt (g e j) c -> p (kt g) e j c", e=2, j=4)
                        for e in range(2):
                            ins = nc.scalar.copy(dst[:, :, e, :, 16 * e:16 * e + HEAD], src[:, :, e])
                ins.then_inc(side_read, 1)

            def copy_values(it, k):
                if exists(it, k):
                    act.wait_ge(values_summed, batch(it, k) * QUADS + QUADS)
                    if due(count := side("turn_values", it, k - 1)):
                        act.wait_ge(side_written, count)
                    nc.scalar.copy(valuesT[:], ps_values[:]).then_inc(values_copied, 1)

            def act_batch(it, k):
                for s in range(8):
                    if s == 2:
                        copy_values(it, k - 1)
                    exponentials(it, k, s)
                    side_job(it, k, s)
                    if group := later_group(it, k, s):
                        if group + 1 < GROUPS:
                            load_group(group + 1)
                        take_root(group)
                    if group := later_group(it, k, s - 1):
                        copy_group(group)

            def body(it):
                for k in range(UNROLL):
                    act_batch(it, k)

            rounds(act, body)
            act_batch(ROUNDS, 0)
            act_batch(ROUNDS, 1)

        @block.vector
        def _(dve):
            v = nc.vector
            steps = [0]

            def step(ins):
                steps[0] += 1
                ins.then_inc(dve_step, 1)
                dve.wait_ge(dve_step, steps[0])

            def scales(amax_all, scale, inverse_scale):
                step(v.tensor_scalar(scale, amax_all, 1e-12, None, ALU.max))
                step(v.reciprocal(inverse_scale, scale))
                step(v.tensor_scalar(scale, inverse_scale, FP8_MAX, FP8_MAX, ALU.mult, ALU.min))
                step(v.reciprocal(inverse_scale, scale))

            dve.wait_ge(setup_loaded, 16 * SETUP_LOADS)
            step(v.tensor_reduce(amax_w, raw[:, 4, :], AX.X, ALU.max, apply_absolute_value=True))
            v.tensor_copy(ident16[:], ident)
            v.tensor_copy(identb[:], ident)
            def reorder(dst, src):
                for g in range(2):
                    to = dst[:, 64 * g:64 * g + 64].rearrange("p (j e d) -> p j e d", e=2, j=4)
                    v.tensor_copy(to, src[:, 64 * g:64 * g + 64].rearrange("p (e j d) -> p j e d", e=2, j=4))

            def swap(dst, src):
                v.tensor_copy(swapped(dst)[:, :, 0], swapped(src)[:, :, 1])
                return v.tensor_copy(swapped(dst)[:, :, 1], swapped(src)[:, :, 0])

            reorder(wo_order[:], raw[:, 3, :])
            reorder(bias_rows[:, 2, :], bias_rows[:, 0, :])
            step(swap(bias_rows[:, 1, :], bias_rows[:, 0, :]))
            dve.wait_ge(biases_turned, 1)
            step(v.tensor_copy(bias_cols[:], ps_side[:, 0:9].rearrange("p (a b) -> p a b", a=3)))
            step(v.tensor_copy(bv_wide[:], bias_cols[:, 2, 2:3].to_broadcast([P, P])))
            dve.wait_ge(weights_turned, 1)
            ps = [ps_side[:, i * P:(i + 1) * P] for i in range(4)]
            for w, p in ((wqT, ps[0]), (wkT, ps[1])):
                v.tensor_copy(w[:, 0, :], p)
                swap(w[:, 1, :], p)
            v.tensor_copy(wvT[:], ps[2])
            v.tensor_copy(woT[:], ps[3]).then_inc(weights_ready, 1)
            dve.wait_ge(weight_reduced, 1)
            scales(amax_w_all, scale_w, inv_w)
            y, m, t, z = (quant_w[:, i, :] for i in range(4))
            step(v.tensor_scalar(y, raw[:, 4, :], scale_w, FP8_MAX, ALU.mult, ALU.min))
            step(v.tensor_scalar(z, y, -FP8_MAX, None, ALU.max))
            step(v.tensor_scalar(m.bitcast(I32), z.bitcast(I32), EXPONENT, None, ALU.bitwise_and))
            step(v.tensor_scalar(t, m, TINY, MAGIC, ALU.max, ALU.mult))
            step(v.tensor_tensor(y, z, t, ALU.add))
            v.tensor_tensor(w8[:], y, t, ALU.subtract).then_inc(weight_quantised, 1)
            dve.wait_ge(weight8_turned, 1)
            v.tensor_copy(w8T[:], ps_sideb[:, 0:P])
            step(v.tensor_tensor(bo_rows[:], bo_rows[:], ps_side[:, P:2 * P], ALU.add))
            def norm_group(group):
                r = group % 2
                dve.wait_ge(rows_loaded[r], group // 2 * 16 + 16)
                for i in range(GROUP):
                    ins = v.bn_stats(stats[:, i, :], xg[:, r, i, :])
                step(ins)
                for i in range(GROUP):
                    ins = v.bn_aggr(moments[:, r, i, :], stats[:, i, :])
                step(ins)
                v.tensor_scalar(spread[:, r, :], moments[:, r, :, 1], EPS, None, ALU.add).then_inc(variance_ready, 1)
                dve.wait_ge(root_ready, group + 1)
                step(v.reciprocal(rstd[:, r, :], root[:, r, :]))
                step(v.tensor_tensor(newton[:], rstd[:, r, :], rstd[:, r, :], ALU.mult))
                step(v.tensor_tensor(newton[:], newton[:], spread[:, r, :], ALU.mult))
                step(v.tensor_scalar(newton[:], newton[:], -0.5, 1.5, ALU.mult, ALU.add))
                v.tensor_tensor(rstd[:, r, :], rstd[:, r, :], newton[:], ALU.mult).then_inc(rstd_ready, 1)
                dve.wait_ge(rstd_ready, group + 1)
                if due(count := group - 1):
                    dve.wait_ge(group_turned, count)
                for i in range(GROUP):
                    ins = v.tensor_scalar(xn[:, r, i, :], xg[:, r, i, :], moments[:, r, i, 0:1],
                                          rstd[:, r, i:i + 1], ALU.subtract, ALU.mult)
                ins.then_inc(normalised, 1)

            def group_max(group):
                dve.wait_ge(normalised, group + 1)
                v.tensor_reduce(largest[:, group:group + 1], xn[:, group % 2].rearrange("p a b -> p (a b)"), AX.X, ALU.max,
                                apply_absolute_value=True).then_inc(group_largest, 1)

            norm_group(0)

            def find_scales():
                group_max(GROUPS - 1)
                dve.wait_ge(group_largest, GROUPS)
                v.tensor_reduce(amax_x, largest[:], AX.X, ALU.max).then_inc(largest_ready, 1)
                dve.wait_ge(largest_reduced, 1)
                scales(amax_x_all, scale_x, inv_x)
                step(v.tensor_tensor(unscale, inv_x, inv_w, ALU.mult))

            def row_maxima(it, k, s):
                ka, u = k + 1 + (s + LEAD) // 8, (s + LEAD) % 8
                if not exists(it, ka):
                    return
                done = batch(it, ka) * 8 + u
                if u == 0:
                    if due(count := side("turn_maxima", it, ka - 2)):
                        dve.wait_ge(side_written, count)
                dve.wait_ge(rows_scored, done + 1)
                v.tensor_reduce(maxima[:, ka % 2, u % 2, 4 * (u // 2):4 * (u // 2) + 4], ps_rows[u % 2][:],
                                AX.X, ALU.max, negate=True).then_inc(rows_reduced, 1)

            def side_job(it, k, s):
                name, ahead = (ODD if k % 2 else EVEN).get(s, (None, 0))
                j = k + ahead
                if name in (None, "v", "turn_maxima", "turn_heads") or not exists(it, j):
                    return
                dve.wait_ge(side_written, side(name, it, j))
                if name == "turn_values":
                    groups = ps_side[:].rearrange("p (h c) -> p h c", c=16)
                    v.reciprocal(inverse[:], groups[:, :, 8]).then_inc(sums_inverted, 1)
                    dve.wait_ge(sums_inverted, batch(it, j) + 1)
                    if due(count := side("turn_heads", it, j - 1)):
                        dve.wait_ge(side_written, count)
                    factor = inverse[:].rearrange("p (h one) -> p h one", one=1).to_broadcast([P, 32, HEAD])
                    ins = v.tensor_tensor(heads[:].rearrange("p (h d) -> p h d", d=HEAD), groups[:, :, 0:HEAD],
                                          factor, ALU.mult)
                elif name == "out":
                    if due(count := batch(it, j)):
                        dve.wait_ge(result_ready, count)
                    dve.wait_ge(x_bias_ready, batch(it, j) + 1)
                    bias = bf_rows[:].rearrange("p (one d) -> p one d", one=1).to_broadcast([P, 2, P])
                    both = ps_side[:].rearrange("p (a t d) -> p a t d", a=2, t=2)
                    v.scalar_tensor_tensor(ffn[:], both[:, 1], unscale, bias, ALU.mult, ALU.add)
                    ins = v.tensor_tensor(attn[:], both[:, 0], x_bias[:], ALU.add)
                else:
                    c, half = int(name[0] == "k"), int(name.endswith("swapped"))
                    if due(count := (it * 2 + j // 2) * 2 + c - 1):
                        dve.wait_ge(pool_rotated, count)
                    wave = (cos, sin)[half].rearrange("p (one w) -> p one w", one=1).to_broadcast([P, 2, SEQ])
                    ins = v.scalar_tensor_tensor(
                        turned[:, c, half].rearrange("p (b w) -> p b w", b=2),
                        ps_side[:].rearrange("p (b w) -> p b w", b=2), bias_cols[:, half, c:c + 1],
                        wave, ALU.add, ALU.mult)
                ins.then_inc(side_read, 1)

            def scale_x8(it, k):
                if not exists(it, k):
                    return
                dve.wait_ge(group_copied, it + k // 4 + 1)
                if due(count := batch(it, k)):
                    dve.wait_ge(x8_sum_ready, count)
                v.tensor_scalar(x8_scaled[:], xnT[:, bass.ds(batch(it, k) * SEQ, SEQ)], scale_x, FP8_MAX,
                                ALU.mult, ALU.min).then_inc(x8_scaled_ready, 1)
                dve.wait_ge(x8_scaled_ready, batch(it, k) + 1)
                v.tensor_scalar(x8_magic[:, 0, :].bitcast(I32), x8_scaled[:].bitcast(I32), EXPONENT, None,
                                ALU.bitwise_and).then_inc(x8_exponent_ready, 1)

            def dve_batch(it, k):
                for s in range(8):
                    row_maxima(it, k, s)
                    side_job(it, k, s)
                    if s == 6:
                        scale_x8(it, k)
                    if group := later_group(it, k, s):
                        norm_group(group)
                        group_max(group - 1)
                    if lead_in(it) and k == 2 and s == 0:
                        find_scales()

            def body(it):
                for k in range(UNROLL):
                    dve_batch(it, k)

            rounds(dve, body)
            dve_batch(ROUNDS, 0)
            dve_batch(ROUNDS, 1)

        @block.tensor
        def _(pe):
            mm = nc.tensor.matmul
            pe.wait_ge(dve_step, 2)
            for i in range(3):
                ins = nc.tensor.transpose(ps_side[:, 3 * i:3 * i + 3], bias_rows[:, i, :], ident[0:3, 0:3])
            ins.then_inc(biases_turned, 1)
            pe.wait_ge(dve_step, 3)
            for i in range(3):
                nc.tensor.transpose(ps_side[:, i * P:(i + 1) * P], raw[:, i, :], ident)
            nc.tensor.transpose(ps_side[:, 3 * P:4 * P], wo_order[:], ident).then_inc(weights_turned, 1)
            pe.wait_ge(weights_ready, 1)
            pe.wait_ge(weight_quantised, 1)
            nc.tensor.transpose(ps_sideb[:, 0:P], w8[:], identb[:])
            mm(ps_side[:, P:2 * P], bv_wide[:], woT[:], start=True, stop=True).then_inc(weight8_turned, 1)

            def turn_group(group):
                r = group % 2
                pe.wait_ge(normalised, group + 1)
                if due(count := group - 1):
                    pe.wait_ge(group_copied, count)
                for i in range(GROUP):
                    ins = nc.tensor.transpose(ps_rows[r][:].rearrange("p a b -> p (a b)")[:, i * P:(i + 1) * P],
                                              xn[:, r, i, :], ident)
                ins.then_inc(group_turned, 1)

            turn_group(0)

            def score_rows(it, k, s):
                ka, u = k + 1 + (s + LEAD) // 8, (s + LEAD) % 8
                if not exists(it, ka):
                    return
                done, buf = batch(it, ka) * 8 + u, ka % UNROLL
                t, half = u // 2, u % 2
                if u == 0:
                    pe.wait_ge(stack_loaded[buf], (it + ka // 4 + 1) * 80)
                if isinstance(it, int) and batch(it, ka) == 0 and u == 0:
                    pe.wait_ge(group_copied, GROUPS)
                if due(count := done - 1):
                    pe.wait_ge(rows_reduced, count)
                for a in range(2):
                    ins = mm(ps_rows[u % 2][:, 2 * a:2 * a + 2, :], q_stack[:, buf, t, half * P:(half + 1) * P],
                             k_stack[:, buf, 4 * t + 2 * a:4 * t + 2 * a + 2, :], start=True, stop=True)
                ins.then_inc(rows_scored, 1)

            def score_cols(it, k, s):
                if not exists(it, k):
                    return
                buf = k % UNROLL
                if s == 0:
                    pe.wait_ge(shift_loaded[buf], (it + k // 4 + 1) * 64)
                for h in (2 * s, 2 * s + 1):
                    done = batch(it, k) * HEADS + h
                    if due(count := done - 1):
                        pe.wait_ge(probs_ready, count)
                    for kt in range(2):
                        ins = mm(ps_cols[h % 2][:, kt * SEQ:(kt + 1) * SEQ], k_stack[:, buf, h, kt * P:(kt + 1) * P],
                                 q_stack[:, buf, h // 4, :], start=True, stop=True)
                    ins.then_inc(cols_scored, 1)

            def sum_values(it, k, s):
                k, s = (k, s - 2) if s >= 2 else (k - 1, s + 6)
                if not exists(it, k):
                    return
                buf, t, kt = k % UNROLL, s // 2, s % 2
                g, e = t // 2, t % 2
                if kt == 0:
                    pe.wait_ge(probs_ready, batch(it, k) * HEADS + 4 * t + 4)
                if s == 0:
                    if due(count := batch(it, k)):
                        pe.wait_ge(values_copied, count)
                    pe.wait_ge(side_read, side("v", it, k - k % 2))
                for j in range(4):
                    h = 4 * t + j
                    ins = mm(ps_values[32 * j:32 * j + 32, g * SEQ:(g + 1) * SEQ], v_pad[:, buf, kt, h, :],
                             probs[:, h % 8, kt * SEQ:(kt + 1) * SEQ],
                             start=(e == 0 and kt == 0), stop=(e == 1 and kt == 1))
                if kt == 1:
                    ins.then_inc(values_summed, 1)

            def side_job(it, k, s):
                name, ahead = (ODD if k % 2 else EVEN).get(s, (None, 0))
                j = k + ahead
                if name is None or not exists(it, j):
                    return
                if due(count := side(name, it, j) - 1):
                    pe.wait_ge(side_read, count)
                r = (j // 2) % 2
                if name[0] in "qk":
                    w = (wqT, wkT)[int(name[0] == "k")]
                    pe.wait_ge(xc_loaded[r], (it + j // 4 + 1) * 16)
                    ins = mm(ps_side[:], w[:, int(name.endswith("swapped")), :], xc[:, r, :], start=True, stop=True)
                elif name == "v":
                    pe.wait_ge(xc_loaded[r], (it + j // 4 + 1) * 16)
                    for i in range(4):
                        ins = mm(ps_side[:, i * P:(i + 1) * P], xc[:, r, i * P:(i + 1) * P], wvT[:],
                                 start=True, stop=True)
                elif name == "turn_maxima":
                    pe.wait_ge(rows_reduced, batch(it, j) * 8 + 8)
                    for half in range(2):
                        ins = nc.tensor.transpose(ps_side16[0:HEADS, half * P:(half + 1) * P],
                                                  maxima[:, j % 2, half, :], ident16[:])
                elif name == "turn_values":
                    pe.wait_ge(values_copied, batch(it, j) + 1)
                    for g in range(2):
                        for half in range(2):
                            to = (2 * half + g) * P
                            ins = nc.tensor.transpose(ps_side[:, to:to + P],
                                                      valuesT[:, g * SEQ + half * P:g * SEQ + (half + 1) * P], ident)
                elif name == "turn_heads":
                    pe.wait_ge(side_read, side("turn_values", it, j))
                    for half in range(2):
                        ins = nc.tensor.transpose(ps_side[:, half * P:(half + 1) * P],
                                                  heads[:, half * P:(half + 1) * P], ident)
                else:
                    pe.wait_ge(side_read, side("turn_heads", it, j))
                    pe.wait_ge(x8_ready, batch(it, j) + 1)
                    for half in range(2):
                        mm(ps_side[:, half * P:(half + 1) * P], headsT[:, half * P:(half + 1) * P], woT[:],
                           start=True, stop=True)
                    for half in range(2):
                        ins = mm(ps_side[:, SEQ + half * P:SEQ + (half + 1) * P], x8[:, j % 2, half * P:(half + 1) * P],
                                 w8T[:], start=True, stop=True)
                ins.then_inc(side_written, 1)

            def pe_batch(it, k):
                for s in range(8):
                    score_rows(it, k, s)
                    score_cols(it, k, s)
                    sum_values(it, k, s)
                    side_job(it, k, s)
                    if group := later_group(it, k, s - 1):
                        turn_group(group)

            def body(it):
                for k in range(UNROLL):
                    pe_batch(it, k)

            rounds(pe, body)
            pe_batch(ROUNDS, 0)
            pe_batch(ROUNDS, 1)


_INS = ["L0_attn_x", "L0_attn_Wq", "L0_attn_bq", "L0_attn_Wk", "L0_attn_bk", "L0_attn_Wv", "L0_attn_bv",
        "L0_attn_Wo", "L0_attn_bo", "L0_ffn_weight", "L0_ffn_bias"]


def constant_tables():
    import numpy as np

    half = P // 2
    steps = np.arange(half, dtype=np.float32) / np.float32(half)
    frequency = np.float32(1.0) / np.power(np.float32(10000.0), steps, dtype=np.float32)
    angle = np.arange(SEQ, dtype=np.float32)[None, :] * frequency[:, None]
    t = np.zeros((P, T_COLS), np.float32)
    t[:, T_ID:T_ID + P] = np.eye(P, dtype=np.float32)
    t[:, T_COS:T_COS + SEQ] = np.repeat(np.cos(angle, dtype=np.float32), 2, axis=0)
    t[:, T_SIN:T_SIN + SEQ] = np.repeat(np.sin(angle, dtype=np.float32), 2, axis=0)
    t[0::2, T_SIN:T_SIN + SEQ] *= np.float32(-1.0)
    t[0::HEAD, T_FLAG] = 1.0
    return t


def kernel(**inputs):
    import numpy as np
    from concourse import bacc
    from concourse.bass_utils import run_bass_kernel_spmd

    nc = bacc.Bacc("TRN2", target_bir_lowering=False, num_devices=1)
    arrays = {"tables": constant_tables()}
    args = [nc.dram_tensor("tables", (P, T_COLS), F32, kind="ExternalInput").ap()]
    for name in _INS:
        a = np.ascontiguousarray(inputs[name])
        arrays[f"in_{name}"] = a
        args.append(nc.dram_tensor(f"in_{name}", a.shape, mybir.dt.from_np(a.dtype), kind="ExternalInput").ap())
    out = nc.dram_tensor("out", (BATCH, SEQ, P), F32, kind="ExternalOutput").ap()
    attention_and_ffn(nc, *args, out)
    r = run_bass_kernel_spmd(nc, [arrays], core_ids=[0])
    return r.results[0]["out"]
```

```python
from contextlib import ExitStack

import concourse.bass as bass
from concourse import mybir

ALU = mybir.AluOpType
ACT = mybir.ActivationFunctionType
AX = mybir.AxisListType
F32 = mybir.dt.float32
F16 = mybir.dt.float16
BF16 = mybir.dt.bfloat16
I32 = mybir.dt.int32

P = 128
BATCH, SEQ, HEADS = 32, 256, 16
HEAD = P // HEADS
TILES = BATCH * SEQ // P
QUADS = HEADS // 4
SCALE = HEAD ** -0.5
EPS = 1e-5
FP8_MAX = 448.0
MAGIC = 1.5 * 2.0 ** 20
TINY = 2.0 ** -6
EXPONENT = 0x7F800000
LEAD = 5
UNROLL = 4
ROUNDS = BATCH // UNROLL
GROUP = 8
GROUPS = TILES // GROUP
GROUP_BUFS = 4
POOL_TILES = 3
T_ID, T_COS, T_SIN, T_FLAG = 0, P, P + SEQ, P + 3 * SEQ
T_COLS = T_FLAG + 1

EVEN = {1: ("turn_heads", -2), 2: ("out", -2), 4: ("turn_maxima", 1), 5: ("turn_values", -1), 6: ("k", 4)}
ODD = {1: ("turn_heads", -2), 2: ("out", -2), 3: ("v", 1), 4: ("turn_maxima", 1), 5: ("turn_values", -1),
       6: ("q", 5)}

LATER_GROUPS = {(-4, 1): 2, (-4, 3): 3, (-4, 5): 4, (-4, 6): 5, (-4, 7): 6, (-3, 0): 7}

FIRST_JOBS = {(-4, 2): ("q", 0), (-4, 4): ("k", 0), (-2, 3): ("q", 2), (-2, 5): ("k", 2), (-1, 1): ("v", 0),
              (-1, 4): ("turn_maxima", 0), (-1, 6): ("q", 4)}


def job_at(n, k, s):
    if n is not None and n < 0:
        name, j = FIRST_JOBS.get((n, s), (None, 0))
        return name, j - n
    return (ODD if k % 2 else EVEN).get(s, (None, 0))


def plan_side_jobs():
    at = {}
    for n in range(-4, BATCH + 2):
        for s in range(8):
            name, ahead = job_at(n, n, s)
            if name and 0 <= n + ahead < BATCH:
                at[name, n + ahead] = len(at)
    return at


def attention_and_ffn(nc, tables, x, wq, bq, wk, bk, wv, bv, wo, bo, wf, bf, out):
    side_at = plan_side_jobs()
    per_round = len(EVEN) * 2 + len(ODD) * 2

    def exists(it, k):
        return not isinstance(it, int) or 0 <= UNROLL * it + k < BATCH

    def batch(it, k):
        return it * UNROLL + k

    def job(it, k, s):
        return job_at(UNROLL * it + k if isinstance(it, int) else None, k, s)

    def earlier(k, s, slots):
        return (k, s - slots) if s >= slots else (k - 1, s - slots + 8)

    def lead_in(it):
        return isinstance(it, int) and it < 0

    def later_group(it, k, s):
        return LATER_GROUPS.get((UNROLL * it + k, s)) if lead_in(it) else None

    def side(name, it, k):
        if isinstance(it, int):
            return side_at.get((name, UNROLL * it + k), -1) + 1
        first = side_at[name, UNROLL + k]
        for r in range(1, ROUNDS - 2):
            assert side_at[name, UNROLL * r + k] == first + per_round * (r - 1)
        return it * per_round + (first - per_round + 1)

    def due(count):
        return not isinstance(count, int) or count > 0

    def pass_wait(engine, semaphore):
        engine.sem_inc(semaphore, 1)

    def rounds(engine, body):
        body(-1)
        body(0)
        with engine.Fori(1, ROUNDS - 2) as it:
            body(it)
        body(ROUNDS - 2)
        body(ROUNDS - 1)

    with ExitStack() as ctx:
        def sbuf(name, shape, dt):
            return ctx.enter_context(nc.sbuf_tensor(name, shape, dt))

        def psum(name, shape, dt):
            return ctx.enter_context(nc.psum_tensor(name, shape, dt))

        def sem(name):
            return ctx.enter_context(nc.semaphore(name))

        scratch = [[nc.dram_tensor(f"scratch_{n}{r}", [P, 2, 4, SEQ], F16, kind="Internal").ap()
                    for r in range(2)] for n in "qk"]

        table = sbuf("table", [P, T_COLS], F32)
        ident = table[:, T_ID:T_ID + P]
        ident16 = sbuf("ident16", [P, P], F16)
        identb = sbuf("identb", [P, P], BF16)
        raw = sbuf("raw", [P, 5, P], F32)
        wo_order = sbuf("wo_order", [P, P], F32)
        wqT = sbuf("wqT", [P, P], F32)
        wkT = sbuf("wkT", [P, P], F32)
        wvT = sbuf("wvT", [P, P], F32)
        woT = sbuf("woT", [P, P], F32)
        w8 = sbuf("w8", [P, P], BF16)
        w8T = sbuf("w8T", [P, P], BF16)
        bias_rows = sbuf("bias_rows", [3, 4, P], F32)
        bias_cols = sbuf("bias_cols", [P, 3, 3], F32)
        bv_wide = sbuf("bv_wide", [P, P], F32)
        bo_rows = sbuf("bo_rows", [P, P], F32)
        bf_rows = sbuf("bf_rows", [P, P], F32)
        small = sbuf("small", [P, 16], F32)
        quant_w = sbuf("quant_w", [P, 4, P], F32)
        fill = sbuf("fill", [P, 2, 2 * SEQ], F16)

        xg = sbuf("xg", [P, GROUP_BUFS, GROUP, P], F32)
        xn = sbuf("xn", [P, 2, GROUP, P], F32)
        stats = sbuf("stats", [P, 2, GROUP, 6], F32)
        moments = sbuf("moments", [P, 2, GROUP, 2], F32)
        spread = sbuf("spread", [P, 2, GROUP], F32)
        root = sbuf("root", [P, 2, GROUP], F32)
        rstd = sbuf("rstd", [P, 2, GROUP], F32)
        newton = sbuf("newton", [P, GROUP], F32)
        largest = sbuf("largest", [P, GROUPS], F32)
        xnT = sbuf("xnT", [P, BATCH * SEQ], F32)

        xc = sbuf("xc", [P, 2, 2 * SEQ], F32)
        turned = sbuf("turned", [P, 2, 3, 2 * SEQ], F32)
        rotated = sbuf("rotated", [P, 2 * SEQ], F32)
        parts = sbuf("parts", [P, 2, 2, 2, SEQ], F16)
        q_stack = sbuf("q_stack", [P, UNROLL, QUADS, SEQ], F16)
        k_stack = sbuf("k_stack", [P, UNROLL, HEADS, SEQ], F16)
        maxima = sbuf("maxima", [P, 2, 2, HEADS], F16)
        max_rows = sbuf("max_rows", [HEADS, 2, SEQ], F16)
        probs = sbuf("probs", [P, 8, 2 * SEQ], F32)
        v_pad = sbuf("v_pad", [P, UNROLL, 2, HEADS, 32], F32)
        valuesT = sbuf("valuesT", [P, 2 * SEQ], F32)
        inverse = sbuf("inverse", [P, 32], F32)
        heads = sbuf("heads", [P, SEQ], F32)
        headsT = sbuf("headsT", [P, SEQ], F32)
        x8_scaled = sbuf("x8_scaled", [P, SEQ], F32)
        x8_clipped = sbuf("x8_clipped", [P, SEQ], F32)
        x8_magic = sbuf("x8_magic", [P, 2, SEQ], F32)
        x8_sum = sbuf("x8_sum", [P, SEQ], F32)
        x8 = sbuf("x8", [P, 2, SEQ], BF16)
        x_rows = sbuf("x_rows", [P, 2, 2, P], F32)
        x_bias = sbuf("x_bias", [P, 2, P], F32)
        ffn = sbuf("ffn", [P, 2, P], BF16)
        attn = sbuf("attn", [P, 2, P], F32)
        result = sbuf("result", [P, 2, 2, P], F32)

        ps_rows = [psum(f"ps_rows{r}", [P, 4, SEQ], F32) for r in range(2)]
        ps_cols = [psum(f"ps_cols{r}", [P, 2 * SEQ], F32) for r in range(2)]
        ps_values = psum("ps_values", [P, 2 * SEQ], F32)
        ps_side = psum("ps_side", [P, 2 * SEQ], F32)
        ps_side16 = ps_side[:].bitcast(F16)
        ps_sideb = ps_side[:].bitcast(BF16)

        setup_loaded = sem("setup_loaded")
        dve_step = sem("dve_step")
        stacks_cleared = sem("stacks_cleared")
        weight_largest = sem("weight_largest")
        biases_ready = sem("biases_ready")
        bias_cols_ready = sem("bias_cols_ready")
        stats_ready = sem("stats_ready")
        pool_filled = sem("pool_filled")
        biases_turned = sem("biases_turned")
        weights_turned = sem("weights_turned")
        weights_ready = sem("weights_ready")
        fill_stored = sem("fill_stored")
        weight_reduced = sem("weight_reduced")
        weight_quantised = sem("weight_quantised")
        weight8_turned = sem("weight8_turned")
        bias_summed = sem("bias_summed")
        rows_loaded = [sem(f"rows_loaded{r}") for r in range(GROUP_BUFS)]
        variance_ready = sem("variance_ready")
        root_ready = sem("root_ready")
        rstd_ready = sem("rstd_ready")
        normalised = sem("normalised")
        pool_normalised = sem("pool_normalised")
        group_largest = sem("group_largest")
        wide_ready = sem("wide_ready")
        setup_read = sem("setup_read")
        group_turned = sem("group_turned")
        group_copied = sem("group_copied")
        largest_ready = sem("largest_ready")
        largest_reduced = sem("largest_reduced")
        scales_ready = sem("scales_ready")

        sp_passed, pool_passed, dve_passed = sem("sp_passed"), sem("pool_passed"), sem("dve_passed")

        xc_loaded = [sem(f"xc_loaded{r}") for r in range(2)]
        side_written = sem("side_written")
        side_read = sem("side_read")
        products_ready = sem("products_ready")
        pool_rotated = sem("pool_rotated")
        high_cut = sem("high_cut")
        low_cut = sem("low_cut")
        parts_stored = [sem(f"parts_stored{c}") for c in "qk"]
        stack_loaded = [sem(f"stack_loaded{r}") for r in range(UNROLL)]
        shift_loaded = [[sem(f"shift_loaded{t}{r}") for r in range(2)] for t in range(QUADS)]
        rows_scored = sem("rows_scored")
        rows_reduced = sem("rows_reduced")
        cols_scored = sem("cols_scored")
        probs_ready = sem("probs_ready")
        values_summed = sem("values_summed")
        values_copied = sem("values_copied")
        sums_inverted = sem("sums_inverted")
        x8_scaled_ready = sem("x8_scaled_ready")
        x8_exponent_ready = sem("x8_exponent_ready")
        x8_clipped_ready = sem("x8_clipped_ready")
        x8_magic_ready = sem("x8_magic_ready")
        x8_sum_ready = sem("x8_sum_ready")
        x8_ready = sem("x8_ready")
        x_loaded = [sem(f"x_loaded{r}") for r in range(2)]
        x_bias_ready = sem("x_bias_ready")
        result_ready = sem("result_ready")
        stored = [sem(f"stored{r}") for r in range(2)]

        amax_w, amax_w_all, scale_w, inv_w = (small[:, i:i + 1] for i in range(4))
        amax_x, amax_x_all, scale_x, inv_x = (small[:, i:i + 1] for i in range(4, 8))
        unscale = small[:, 8:9]
        SETUP_LOADS = 11

        def even_first(ap):
            return ap.rearrange("p (i two) -> p two i", two=2)

        block = ctx.enter_context(nc.Block())

        @block.sync
        def _(sp):
            sp.dma_start(table[:], tables).then_inc(setup_loaded, 16)
            for i, w in enumerate((wq, wk, wv, wo, wf)):
                sp.dma_start(raw[:, i, :], w).then_inc(setup_loaded, 16)
            for i, b in enumerate((bq, bk, bv)):
                sp.dma_start(bias_rows[i:i + 1, 0, :], b.rearrange("(one f) -> one f", one=1)).then_inc(setup_loaded, 16)
            sp.dma_start(bo_rows[:], bo.partition_broadcast(P)).then_inc(setup_loaded, 16)
            sp.dma_start(bf_rows[:], bf.partition_broadcast(P)).then_inc(setup_loaded, 16)

            sp.wait_ge(pool_filled, 5)
            for c in range(2):
                for r in range(2):
                    sp.dma_start(scratch[c][r][:, :, 3, :], fill[:, c, :].rearrange("p (two w) -> p two w", two=2))\
                      .then_inc(fill_stored, 16)
            sp.wait_ge(fill_stored, 64)

            def load_xc(it, k):
                if exists(it, k):
                    r = (k // 2) % 2
                    sp.wait_ge(group_copied, it + k // 4 + 1)
                    pass_wait(sp, sp_passed)
                    if due(count := side("v", it, k - 4)):
                        sp.wait_ge(side_written, count)
                        pass_wait(sp, sp_passed)
                    src = xnT[:, bass.ds(batch(it, k) * SEQ, 2 * SEQ)]
                    sp.dma_start(xc[:, r, :], src).then_inc(xc_loaded[r], 16)

            def store_parts(c, it, k):
                if not exists(it, k):
                    return
                r = (k // 2) % 2
                pair = it * 2 + k // 2
                for b in range(2):
                    if due(count := (it + (k - 4) // 4 + 1) * 80):
                        sp.wait_ge(stack_loaded[(k + b) % UNROLL], count)
                        pass_wait(sp, sp_passed)
                sp.wait_ge(low_cut, pair * 2 + c + 1)
                pass_wait(sp, sp_passed)
                one, two = (slice(0, 1), slice(1, 3)) if c == 0 else (slice(2, 3), slice(0, 2))
                sp.dma_start(scratch[c][r][:, :, one], parts[:, c, :, 0:1]).then_inc(parts_stored[c], 16)
                sp.dma_start(scratch[c][r][:, :, two], parts[:, c]).then_inc(parts_stored[c], 16)

            def load_stacks(it, k):
                if not exists(it, k):
                    return
                r, b, buf = (k // 2) % 2, k % 2, k % UNROLL
                pair = it * 2 + k // 2
                if due(count := (batch(it, k) - 3) * HEADS):
                    sp.wait_ge(cols_scored, count)
                    pass_wait(sp, sp_passed)
                sp.wait_ge(parts_stored[0], pair * 32 + 32)
                pass_wait(sp, sp_passed)
                src = scratch[0][r].rearrange("(b t f) two c w -> b (f two c) t w", b=2, t=QUADS)
                sp.dma_start(q_stack[:, buf], src[b]).then_inc(stack_loaded[buf], 16)
                sp.wait_ge(parts_stored[1], pair * 32 + 32)
                pass_wait(sp, sp_passed)
                src = scratch[1][r].rearrange("(b t f) two c w -> b (f two c) t w", b=2, t=QUADS)
                sp.wait_ge(stacks_cleared, 1)
                for j in range(4):
                    rows = slice(32 * j, 32 * j + 32)
                    sp.dma_start(k_stack[rows, buf, j:HEADS:4, :], src[b, rows])\
                      .then_inc(stack_loaded[buf], 16)

            def load_shift(it, k):
                if not exists(it, k):
                    return
                buf = k % UNROLL
                sp.wait_ge(side_read, side("turn_maxima", it, k))
                pass_wait(sp, sp_passed)
                for t in range(QUADS):
                    sp.dma_start(q_stack[3:P:32, buf, t, :], max_rows[4 * t:4 * t + 4, k % 2, :])\
                      .then_inc(shift_loaded[t][k % 2], 16)

            def store_result(it, k):
                if exists(it, k):
                    sp.wait_ge(result_ready, batch(it, k) + 1)
                    pass_wait(sp, sp_passed)
                    dst = out[bass.ds(batch(it, k), 1)].rearrange("o (t p) d -> p (o t) d", p=P)
                    sp.dma_start(dst, result[:, k % 2]).then_inc(stored[k % 2], 16)

            def load_x(it, k):
                if exists(it, k):
                    if due(count := batch(it, k) - 1):
                        sp.wait_ge(x_bias_ready, count)
                        pass_wait(sp, sp_passed)
                    src = x[bass.ds(batch(it, k), 1)].rearrange("o (t p) d -> p (o t) d", p=P)
                    sp.dma_start(x_rows[:, k % 2], src).then_inc(x_loaded[k % 2], 16)

            def body(it):
                for k in range(0, UNROLL, 2):
                    if not (lead_in(it) and k == 2):
                        load_xc(it, k + 4)
                    if lead_in(it) and k == 0:
                        load_xc(it, k + 6)
                    store_parts(1, it, k + 2)
                    load_shift(it, k)
                    load_x(it, k - 1)
                    store_result(it, k - 3)
                    load_stacks(it, k + 2)
                    load_stacks(it, k + 3)
                    store_parts(0, it, k + 4)
                    load_shift(it, k + 1)
                    load_x(it, k)
                    store_result(it, k - 2)

            rounds(sp, body)
            load_x(ROUNDS, -1)
            for k in (-3, -2, -1):
                store_result(ROUNDS, k)
            for r in range(2):
                sp.wait_ge(stored[r], BATCH // 2 * 16)

        @block.gpsimd
        def _(pool):
            g = nc.gpsimd
            g.memset(k_stack[:, 2:4].bitcast(F32), 0.0).then_inc(pool_filled, 1)
            g.memset(v_pad[:], 0.0).then_inc(pool_filled, 1)
            pool.wait_ge(pool_filled, 2)
            quads = v_pad[:].rearrange("p b kt (g e j) c -> p (b kt g) e j c", e=2, j=4)
            for e in range(2):
                g.memset(quads[:, :, e, :, 16 * e + 8], 1.0).then_inc(pool_filled, 1)

            def normalise(group):
                r = group % 2
                pool.wait_ge(rstd_ready, group + 1)
                if due(count := group - 1):
                    pool.wait_ge(group_turned, count)
                if due(count := group - 1):
                    pool.wait_ge(group_largest, count)
                for i in range(GROUP - POOL_TILES, GROUP):
                    ins = g.tensor_scalar(xn[:, r, i, :], xg[:, group % GROUP_BUFS, i, :], moments[:, r, i, 0:1],
                                          rstd[:, r, i:i + 1], ALU.subtract, ALU.mult)
                ins.then_inc(pool_normalised, 1)

            normalise(0)
            pool.wait_ge(setup_loaded, 16 * SETUP_LOADS)
            g.memset(fill[:, 0, :], 0.0)
            g.memset(fill[:, 1, SEQ:2 * SEQ], 0.0)
            g.tensor_scalar(fill[:, 1, 0:SEQ], table[:, T_FLAG:T_FLAG + 1].to_broadcast([P, SEQ]), 1.0, None,
                            ALU.mult).then_inc(pool_filled, 1)
            pool.wait_ge(weight_largest, 1)
            g.partition_all_reduce(amax_w_all, amax_w, P, bass.bass_isa.ReduceOp.absmax).then_inc(weight_reduced, 1)
            normalise(1)
            normalise(2)

            def cut(c, it, k):
                if not exists(it, k):
                    return
                done = (it * 2 + k // 2) * 2 + c
                pool.wait_ge(products_ready, done + 1)
                if due(count := done):
                    pool.wait_ge(low_cut, count)
                g.tensor_tensor(rotated[:], turned[:, c, 1, :], turned[:, c, 2, :], ALU.add).then_inc(pool_rotated, 1)
                pool.wait_ge(pool_rotated, done + 1)
                if due(count := (it * 2 + k // 2) * 32):
                    pool.wait_ge(parts_stored[c], count)
                pass_wait(pool, pool_passed)
                whole = rotated[:].rearrange("p (two w) -> p two w", two=2)
                g.tensor_scalar(parts[:, c, :, 0], whole, 1.0, None, ALU.mult).then_inc(high_cut, 1)
                pool.wait_ge(high_cut, done + 1)
                g.tensor_tensor(parts[:, c, :, 1], whole, parts[:, c, :, 0], ALU.subtract).then_inc(low_cut, 1)

            def add_bias(it, k):
                if exists(it, k):
                    pool.wait_ge(x_loaded[k % 2], (it * 2 + k // 2 + 1) * 16)
                    if due(count := side("out", it, k - 1)):
                        pool.wait_ge(side_read, count)
                    bias = bo_rows[:].rearrange("p (one d) -> p one d", one=1).to_broadcast([P, 2, P])
                    g.tensor_tensor(x_bias[:], x_rows[:, k % 2], bias, ALU.add).then_inc(x_bias_ready, 1)

            def quantise(it, k):
                if not exists(it, k):
                    return
                n = batch(it, k) + 1
                if due(count := n - 1):
                    pool.wait_ge(x8_ready, count)
                pool.wait_ge(x8_exponent_ready, n)
                pass_wait(pool, pool_passed)
                g.tensor_scalar(x8_magic[:, 1, :], x8_magic[:, 0, :], TINY, MAGIC, ALU.max, ALU.mult)\
                 .then_inc(x8_magic_ready, 1)
                g.tensor_scalar(x8_clipped[:], x8_scaled[:], -FP8_MAX, None, ALU.max).then_inc(x8_clipped_ready, 1)
                pool.wait_ge(x8_magic_ready, n)
                pool.wait_ge(x8_clipped_ready, n)
                g.tensor_tensor(x8_sum[:], x8_clipped[:], x8_magic[:, 1, :], ALU.add).then_inc(x8_sum_ready, 1)
                pool.wait_ge(x8_sum_ready, n)
                if due(count := side("out", it, k - 2)):
                    pool.wait_ge(side_written, count)
                g.tensor_tensor(x8[:, k % 2, :], x8_sum[:], x8_magic[:, 1, :], ALU.subtract).then_inc(x8_ready, 1)

            def finish(it, k):
                if exists(it, k):
                    pool.wait_ge(side_read, side("out", it, k))
                    if due(count := (it * 2 + k // 2) * 16):
                        pool.wait_ge(stored[k % 2], count)
                    g.tensor_tensor(result[:, k % 2], attn[:], ffn[:], ALU.add).then_inc(result_ready, 1)

            def body(it):
                for k in range(UNROLL):
                    if lead_in(it) and k == 1:
                        normalise(3)
                    if lead_in(it) and k == 2:
                        for group in (4, 5, 6, 7):
                            normalise(group)
                        pool.wait_ge(largest_ready, 1)
                        g.partition_all_reduce(amax_x_all, amax_x, P, bass.bass_isa.ReduceOp.absmax)\
                         .then_inc(largest_reduced, 1)
                    cut(k % 2, it, k + 4 - k % 2)
                    finish(it, k - 2)
                    add_bias(it, k - 1)
                    quantise(it, k)

            rounds(pool, body)
            finish(ROUNDS, -2)
            add_bias(ROUNDS, -1)
            finish(ROUNDS, -1)

        @block.scalar
        def _(act):
            x_tiles = x.rearrange("b (t p) d -> (b t) p d", p=P)

            def load_group(group):
                if due(count := group - GROUP_BUFS + 1):
                    act.wait_ge(normalised, count)
                if due(count := group - GROUP_BUFS + 1):
                    act.wait_ge(pool_normalised, count)
                act.dma_start(xg[:, group % GROUP_BUFS],
                              x_tiles[group * GROUP:(group + 1) * GROUP].rearrange("t p d -> p t d"))\
                   .then_inc(rows_loaded[group % GROUP_BUFS], 16)

            def take_root(group):
                r = group % 2
                act.wait_ge(variance_ready, group + 1)
                nc.scalar.activation(root[:, r, :], spread[:, r, :], ACT.Sqrt).then_inc(root_ready, 1)

            def copy_group(group):
                r = group % 2
                act.wait_ge(group_turned, group + 1)
                nc.scalar.copy(xnT[:, group * GROUP * P:(group + 1) * GROUP * P],
                               ps_rows[r][:].rearrange("p a b -> p (a b)")).then_inc(group_copied, 1)

            for group in range(GROUP_BUFS):
                load_group(group)
            take_root(0)

            act.wait_ge(weights_turned, 1)
            turned_weights = [ps_side[:, i * P:(i + 1) * P] for i in range(4)]
            for w, p in ((wqT, turned_weights[0]), (wkT, turned_weights[1])):
                nc.scalar.copy(w[:].rearrange("p (two i) -> p two i", two=2), even_first(p))
            nc.scalar.copy(wvT[:], turned_weights[2])
            nc.scalar.copy(woT[:], turned_weights[3]).then_inc(weights_ready, 1)
            take_root(1)
            copy_group(0)

            def exponential(it, k, h):
                if not exists(it, k):
                    return
                done = batch(it, k) * HEADS + h
                if h % 4 == 0:
                    if due(count := batch(it, k) * QUADS + h // 4 - 1):
                        act.wait_ge(values_summed, count)
                act.wait_ge(cols_scored, done + 1)
                nc.scalar.activation(probs[:, h % 8, :], ps_cols[h % 2][:], ACT.Exp, scale=SCALE)\
                  .then_inc(probs_ready, 1)

            def side_job(it, k, s):
                name, ahead = job(it, k, s)
                j = k + ahead
                if name not in ("q", "k", "v", "turn_maxima", "turn_heads") or not exists(it, j):
                    return
                act.wait_ge(side_written, side(name, it, j))
                if name in ("q", "k"):
                    c = int(name == "k")
                    if due(count := (it * 2 + j // 2) * 2 + c - 1):
                        act.wait_ge(pool_rotated, count)
                    for two in range(2):
                        cols = slice(two * SEQ, (two + 1) * SEQ)
                        ins = nc.scalar.activation(turned[:, c, 0, cols], ps_side[:, cols], ACT.Identity,
                                                   bias=bias_cols[:, two, c:c + 1])
                elif name == "turn_maxima":
                    ins = nc.scalar.copy(max_rows[:, j % 2, :], ps_side16[0:HEADS, 0:SEQ])
                elif name == "turn_heads":
                    if due(count := side("out", it, j - 1)):
                        act.wait_ge(side_written, count)
                    ins = nc.scalar.copy(headsT[:], ps_side[:, 0:SEQ])
                else:
                    if due(count := (batch(it, j) - 2) * QUADS):
                        act.wait_ge(values_summed, count)
                    act.wait_ge(pool_filled, 5)
                    for b in range(2):
                        src = ps_side[:, b * SEQ:(b + 1) * SEQ].rearrange("p (a e j d) -> p a e j d", e=2, j=4, d=HEAD)
                        dst = v_pad[:, (j + b) % UNROLL].rearrange("p kt (g e j) c -> p (kt g) e j c", e=2, j=4)
                        for e in range(2):
                            ins = nc.scalar.copy(dst[:, :, e, :, 16 * e:16 * e + HEAD], src[:, :, e])
                ins.then_inc(side_read, 1)

            def copy_values(it, k):
                if exists(it, k):
                    act.wait_ge(values_summed, batch(it, k) * QUADS + QUADS)
                    if due(count := side("turn_values", it, k - 1)):
                        act.wait_ge(side_written, count)
                    nc.scalar.copy(valuesT[:], ps_values[:]).then_inc(values_copied, 1)

            def act_batch(it, k):
                for s in range(8):
                    if s == 2:
                        copy_values(it, k - 1)
                    exponential(it, k, 2 * s)
                    exponential(it, k, 2 * s + 1)
                    side_job(it, k, s)
                    if group := later_group(it, k, s):
                        take_root(group)
                        copy_group(group - 1)
                        if GROUP_BUFS <= group + 2 < GROUPS:
                            load_group(group + 2)
                        if group == GROUPS - 1:
                            copy_group(group)

            def body(it):
                for k in range(UNROLL):
                    act_batch(it, k)

            rounds(act, body)
            act_batch(ROUNDS, 0)
            act_batch(ROUNDS, 1)

        @block.vector
        def _(dve):
            v = nc.vector
            steps = [0]

            def step(ins):
                steps[0] += 1
                ins.then_inc(dve_step, 1)
                dve.wait_ge(dve_step, steps[0])

            def begin(ins):
                steps[0] += 1
                ins.then_inc(dve_step, 1)

            def scales(amax_all, scale, inverse_scale):
                step(v.tensor_scalar(scale, amax_all, 1e-12, None, ALU.max))
                step(v.reciprocal(inverse_scale, scale))
                step(v.tensor_scalar(scale, inverse_scale, FP8_MAX, FP8_MAX, ALU.mult, ALU.min))
                step(v.reciprocal(inverse_scale, scale))

            def take_stats(group, tiles):
                for i in tiles:
                    v.bn_stats(stats[:, group % 2, i, :], xg[:, group % GROUP_BUFS, i, :]).then_inc(stats_ready, 1)

            def norm_group(group):
                r = group % 2

                def fill_in(*tiles):
                    if group + 1 < GROUPS:
                        if 0 in tiles:
                            dve.wait_ge(rows_loaded[(group + 1) % GROUP_BUFS], ((group + 1) // GROUP_BUFS + 1) * 16)
                        take_stats(group + 1, tiles)

                if due(count := group - 1):
                    dve.wait_ge(pool_normalised, count)
                dve.wait_ge(stats_ready, group * GROUP + GROUP)
                for i in range(GROUP):
                    ins = v.bn_aggr(moments[:, r, i, :], stats[:, r, i, :])
                step(ins)
                v.tensor_scalar(spread[:, r, :], moments[:, r, :, 1], EPS, None, ALU.add).then_inc(variance_ready, 1)
                fill_in(0, 1, 2, 3)
                dve.wait_ge(root_ready, group + 1)
                begin(v.reciprocal(rstd[:, r, :], root[:, r, :]))
                fill_in(4)
                dve.wait_ge(dve_step, steps[0])
                begin(v.tensor_tensor(newton[:], rstd[:, r, :], rstd[:, r, :], ALU.mult))
                fill_in(5)
                dve.wait_ge(dve_step, steps[0])
                begin(v.tensor_tensor(newton[:], newton[:], spread[:, r, :], ALU.mult))
                fill_in(6)
                dve.wait_ge(dve_step, steps[0])
                begin(v.tensor_scalar(newton[:], newton[:], -0.5, 1.5, ALU.mult, ALU.add))
                dve.wait_ge(dve_step, steps[0])
                v.tensor_tensor(rstd[:, r, :], rstd[:, r, :], newton[:], ALU.mult).then_inc(rstd_ready, 1)
                fill_in(7)
                dve.wait_ge(rstd_ready, group + 1)
                if due(count := group - 1):
                    dve.wait_ge(group_turned, count)
                for i in range(GROUP - POOL_TILES):
                    ins = v.tensor_scalar(xn[:, r, i, :], xg[:, group % GROUP_BUFS, i, :], moments[:, r, i, 0:1],
                                          rstd[:, r, i:i + 1], ALU.subtract, ALU.mult)
                ins.then_inc(normalised, 1)

            def group_max(group):
                dve.wait_ge(normalised, group + 1)
                dve.wait_ge(pool_normalised, group + 1)
                v.tensor_reduce(largest[:, group:group + 1], xn[:, group % 2].rearrange("p a b -> p (a b)"), AX.X,
                                ALU.max, apply_absolute_value=True).then_inc(group_largest, 1)

            v.memset(k_stack[:, 0:2].bitcast(F32), 0.0).then_inc(stacks_cleared, 1)
            dve.wait_ge(rows_loaded[0], 16)
            take_stats(0, range(GROUP))
            norm_group(0)

            dve.wait_ge(setup_loaded, 16 * SETUP_LOADS)
            v.tensor_reduce(amax_w, raw[:, 4, :], AX.X, ALU.max, apply_absolute_value=True).then_inc(weight_largest, 1)
            v.tensor_copy(ident16[:], ident)
            v.tensor_copy(identb[:], ident)
            def reorder(dst, src):
                for g in range(2):
                    to = dst[:, 64 * g:64 * g + 64].rearrange("p (j e d) -> p j e d", e=2, j=4)
                    v.tensor_copy(to, src[:, 64 * g:64 * g + 64].rearrange("p (e j d) -> p j e d", e=2, j=4))

            reorder(wo_order[:], raw[:, 3, :])
            reorder(bias_rows[:, 3, :], bias_rows[:, 0, :])
            for b in range(2):
                ins = v.tensor_copy(bias_rows[:, 1:3, b * P // 2:(b + 1) * P // 2], even_first(bias_rows[:, 0, :]))
            ins.then_inc(biases_ready, 1)
            dve.wait_ge(biases_turned, 1)
            v.tensor_copy(bias_cols[:], ps_side[:, 0:9].rearrange("p (a b) -> p a b", a=3)).then_inc(bias_cols_ready, 1)
            dve.wait_ge(bias_cols_ready, 1)
            v.tensor_copy(bv_wide[:], bias_cols[:, 2, 2:3].to_broadcast([P, P])).then_inc(wide_ready, 1)
            norm_group(1)
            group_max(0)
            dve.wait_ge(weight_reduced, 1)
            scales(amax_w_all, scale_w, inv_w)
            y, m, t, z = (quant_w[:, i, :] for i in range(4))
            step(v.tensor_scalar(y, raw[:, 4, :], scale_w, FP8_MAX, ALU.mult, ALU.min))
            step(v.tensor_scalar(z, y, -FP8_MAX, None, ALU.max))
            step(v.tensor_scalar(m.bitcast(I32), z.bitcast(I32), EXPONENT, None, ALU.bitwise_and))
            step(v.tensor_scalar(t, m, TINY, MAGIC, ALU.max, ALU.mult))
            step(v.tensor_tensor(y, z, t, ALU.add))
            v.tensor_tensor(w8[:], y, t, ALU.subtract).then_inc(weight_quantised, 1)
            dve.wait_ge(weight8_turned, 1)
            v.tensor_copy(w8T[:], ps_sideb[:, 0:P])
            v.tensor_tensor(bo_rows[:], bo_rows[:], ps_side[:, P:2 * P], ALU.add).then_inc(setup_read, 1)
            def find_largest():
                dve.wait_ge(group_largest, GROUPS)
                v.tensor_reduce(amax_x, largest[:], AX.X, ALU.max).then_inc(largest_ready, 1)

            def find_scales():
                dve.wait_ge(largest_reduced, 1)
                scales(amax_x_all, scale_x, inv_x)
                step(v.tensor_tensor(unscale, inv_x, inv_w, ALU.mult))

            def row_maxima(it, k, s):
                ka, u = k + 1 + (s + LEAD) // 8, (s + LEAD) % 8
                if not exists(it, ka):
                    return
                done = batch(it, ka) * 8 + u
                if u == 0:
                    if due(count := side("turn_maxima", it, ka - 2)):
                        dve.wait_ge(side_written, count)
                dve.wait_ge(rows_scored, done + 1)
                v.tensor_reduce(maxima[:, ka % 2, u % 2, 4 * (u // 2):4 * (u // 2) + 4], ps_rows[u % 2][:],
                                AX.X, ALU.max, negate=True).then_inc(rows_reduced, 1)

            def side_job(it, k, s):
                name, ahead = job(it, k, s)
                j = k + ahead
                if name not in ("turn_values", "out") or not exists(it, j):
                    return
                dve.wait_ge(side_written, side(name, it, j))
                if name == "turn_values":
                    groups = ps_side[:].rearrange("p (h c) -> p h c", c=16)
                    v.reciprocal(inverse[:], groups[:, :, 8]).then_inc(sums_inverted, 1)
                    dve.wait_ge(sums_inverted, batch(it, j) + 1)
                    if due(count := side("turn_heads", it, j - 1)):
                        dve.wait_ge(side_written, count)
                    factor = inverse[:].rearrange("p (h one) -> p h one", one=1).to_broadcast([P, 32, HEAD])
                    ins = v.tensor_tensor(heads[:].rearrange("p (h d) -> p h d", d=HEAD), groups[:, :, 0:HEAD],
                                          factor, ALU.mult)
                else:
                    if due(count := batch(it, j)):
                        dve.wait_ge(result_ready, count)
                    dve.wait_ge(x_bias_ready, batch(it, j) + 1)
                    bias = bf_rows[:].rearrange("p (one d) -> p one d", one=1).to_broadcast([P, 2, P])
                    both = ps_side[:].rearrange("p (a t d) -> p a t d", a=2, t=2)
                    v.scalar_tensor_tensor(ffn[:], both[:, 1], unscale, bias, ALU.mult, ALU.add)
                    ins = v.tensor_tensor(attn[:], both[:, 0], x_bias[:], ALU.add)
                ins.then_inc(side_read, 1)

            def multiply_waves(it, k, s):
                k, s = earlier(k, s, 1)
                name, ahead = job(it, k, s)
                j = k + ahead
                if name not in ("q", "k") or not exists(it, j):
                    return
                c = int(name == "k")
                dve.wait_ge(side_read, side(name, it, j))
                q = turned[:, c, 0, :].rearrange("p (two w) -> p two w", two=2)
                v.tensor_tensor(turned[:, c, 1, :].rearrange("p (two w) -> p two w", two=2), q[:, ::-1],
                                table[:, T_SIN:T_SIN + 2 * SEQ].rearrange("p (two w) -> p two w", two=2), ALU.mult)
                cos = table[:, T_COS:T_COS + SEQ].rearrange("p (one w) -> p one w", one=1).to_broadcast([P, 2, SEQ])
                v.tensor_tensor(turned[:, c, 2, :].rearrange("p (two w) -> p two w", two=2), q, cos, ALU.mult)\
                 .then_inc(products_ready, 1)

            def scale_x8(it, k):
                if not exists(it, k):
                    return
                dve.wait_ge(group_copied, it + k // 4 + 1)
                if due(count := batch(it, k)):
                    dve.wait_ge(x8_sum_ready, count)
                v.tensor_scalar(x8_scaled[:], xnT[:, bass.ds(batch(it, k) * SEQ, SEQ)], scale_x, FP8_MAX,
                                ALU.mult, ALU.min).then_inc(x8_scaled_ready, 1)
                dve.wait_ge(x8_scaled_ready, batch(it, k) + 1)
                v.tensor_scalar(x8_magic[:, 0, :].bitcast(I32), x8_scaled[:].bitcast(I32), EXPONENT, None,
                                ALU.bitwise_and).then_inc(x8_exponent_ready, 1)

            def dve_batch(it, k):
                for s in range(8):
                    row_maxima(it, k, s)
                    side_job(it, k, s)
                    multiply_waves(it, k, s)
                    if s == 6:
                        scale_x8(it, k)
                    if group := later_group(it, k, s):
                        norm_group(group)
                        group_max(group - 1)
                        if group == GROUPS - 1:
                            group_max(group)
                            find_largest()
                    if lead_in(it) and k == 2 and s == 5:
                        find_scales()

            def body(it):
                for k in range(UNROLL):
                    dve_batch(it, k)

            rounds(dve, body)
            dve_batch(ROUNDS, 0)
            dve_batch(ROUNDS, 1)

        @block.tensor
        def _(pe):
            mm = nc.tensor.matmul
            def turn_group(group):
                r = group % 2
                pe.wait_ge(normalised, group + 1)
                pe.wait_ge(pool_normalised, group + 1)
                if due(count := group - 1):
                    pe.wait_ge(group_copied, count)
                for i in range(GROUP):
                    ins = nc.tensor.transpose(ps_rows[r][:].rearrange("p a b -> p (a b)")[:, i * P:(i + 1) * P],
                                              xn[:, r, i, :], ident)
                ins.then_inc(group_turned, 1)

            pe.wait_ge(biases_ready, 1)
            for i in range(3):
                ins = nc.tensor.transpose(ps_side[:, 3 * i:3 * i + 3], bias_rows[:, i + 1, :], ident[0:3, 0:3])
            ins.then_inc(biases_turned, 1)
            pe.wait_ge(bias_cols_ready, 1)
            for i in range(3):
                nc.tensor.transpose(ps_side[:, i * P:(i + 1) * P], raw[:, i, :], ident)
            nc.tensor.transpose(ps_side[:, 3 * P:4 * P], wo_order[:], ident).then_inc(weights_turned, 1)
            turn_group(0)
            pe.wait_ge(weights_ready, 1)
            pe.wait_ge(wide_ready, 1)
            pe.wait_ge(weight_quantised, 1)
            nc.tensor.transpose(ps_sideb[:, 0:P], w8[:], identb[:])
            mm(ps_side[:, P:2 * P], bv_wide[:], woT[:], start=True, stop=True).then_inc(weight8_turned, 1)
            pe.wait_ge(setup_read, 1)

            def score_rows(it, k, s):
                ka, u = k + 1 + (s + LEAD) // 8, (s + LEAD) % 8
                if not exists(it, ka):
                    return
                done, buf = batch(it, ka) * 8 + u, ka % UNROLL
                t, half = u // 2, u % 2
                if u == 0:
                    pe.wait_ge(stack_loaded[buf], (it + ka // 4 + 1) * 80)
                if isinstance(it, int) and batch(it, ka) == 0 and u == 0:
                    pe.wait_ge(group_copied, GROUPS)
                if due(count := done - 1):
                    pe.wait_ge(rows_reduced, count)
                for a in range(2):
                    ins = mm(ps_rows[u % 2][:, 2 * a:2 * a + 2, :], q_stack[:, buf, t, half * P:(half + 1) * P],
                             k_stack[:, buf, 4 * t + 2 * a:4 * t + 2 * a + 2, :], start=True, stop=True)
                ins.then_inc(rows_scored, 1)

            def score_cols(it, k, s):
                if not exists(it, k):
                    return
                buf = k % UNROLL
                if s % 2 == 0:
                    pe.wait_ge(shift_loaded[s // 2][k % 2], (it * 2 + k // 2 + 1) * 16)
                for h in (2 * s, 2 * s + 1):
                    done = batch(it, k) * HEADS + h
                    if due(count := done - 1):
                        pe.wait_ge(probs_ready, count)
                    for kt in range(2):
                        ins = mm(ps_cols[h % 2][:, kt * SEQ:(kt + 1) * SEQ], k_stack[:, buf, h, kt * P:(kt + 1) * P],
                                 q_stack[:, buf, h // 4, :], start=True, stop=True)
                    ins.then_inc(cols_scored, 1)

            def sum_values(it, k, s):
                k, s = (k, s - 2) if s >= 2 else (k - 1, s + 6)
                if not exists(it, k):
                    return
                buf, t, kt = k % UNROLL, s // 2, s % 2
                g, e = t // 2, t % 2
                if kt == 0:
                    pe.wait_ge(probs_ready, batch(it, k) * HEADS + 4 * t + 4)
                if s == 0:
                    if due(count := batch(it, k)):
                        pe.wait_ge(values_copied, count)
                    pe.wait_ge(side_read, side("v", it, k - k % 2))
                for j in range(4):
                    h = 4 * t + j
                    ins = mm(ps_values[32 * j:32 * j + 32, g * SEQ:(g + 1) * SEQ], v_pad[:, buf, kt, h, :],
                             probs[:, h % 8, kt * SEQ:(kt + 1) * SEQ],
                             start=(e == 0 and kt == 0), stop=(e == 1 and kt == 1))
                if kt == 1:
                    ins.then_inc(values_summed, 1)

            def side_job(it, k, s):
                name, ahead = job(it, k, s)
                j = k + ahead
                if name is None or not exists(it, j):
                    return
                if due(count := side(name, it, j) - 1):
                    pe.wait_ge(side_read, count)
                r = (j // 2) % 2
                if name in ("q", "k"):
                    w = (wqT, wkT)[int(name == "k")]
                    pe.wait_ge(xc_loaded[r], (it + j // 4 + 1) * 16)
                    for two in range(2):
                        for b in range(2):
                            ins = mm(ps_side[b * P // 2:(b + 1) * P // 2, two * SEQ:(two + 1) * SEQ],
                                     w[:, two * P // 2:(two + 1) * P // 2], xc[:, r, b * SEQ:(b + 1) * SEQ],
                                     start=True, stop=True)
                elif name == "v":
                    pe.wait_ge(xc_loaded[r], (it + j // 4 + 1) * 16)
                    for i in range(4):
                        ins = mm(ps_side[:, i * P:(i + 1) * P], xc[:, r, i * P:(i + 1) * P], wvT[:],
                                 start=True, stop=True)
                elif name == "turn_maxima":
                    pe.wait_ge(rows_reduced, batch(it, j) * 8 + 8)
                    for half in range(2):
                        ins = nc.tensor.transpose(ps_side16[0:HEADS, half * P:(half + 1) * P],
                                                  maxima[:, j % 2, half, :], ident16[:])
                elif name == "turn_values":
                    pe.wait_ge(values_copied, batch(it, j) + 1)
                    for g in range(2):
                        for half in range(2):
                            to = (2 * half + g) * P
                            ins = nc.tensor.transpose(ps_side[:, to:to + P],
                                                      valuesT[:, g * SEQ + half * P:g * SEQ + (half + 1) * P], ident)
                elif name == "turn_heads":
                    pe.wait_ge(side_read, side("turn_values", it, j))
                    for half in range(2):
                        ins = nc.tensor.transpose(ps_side[:, half * P:(half + 1) * P],
                                                  heads[:, half * P:(half + 1) * P], ident)
                else:
                    pe.wait_ge(side_read, side("turn_heads", it, j))
                    pe.wait_ge(x8_ready, batch(it, j) + 1)
                    for half in range(2):
                        mm(ps_side[:, half * P:(half + 1) * P], headsT[:, half * P:(half + 1) * P], woT[:],
                           start=True, stop=True)
                    for half in range(2):
                        ins = mm(ps_side[:, SEQ + half * P:SEQ + (half + 1) * P], x8[:, j % 2, half * P:(half + 1) * P],
                                 w8T[:], start=True, stop=True)
                ins.then_inc(side_written, 1)

            def pe_batch(it, k):
                for s in range(8):
                    score_rows(it, k, s)
                    score_cols(it, k, s)
                    sum_values(it, k, s)
                    side_job(it, k, s)
                    if group := later_group(it, k, s):
                        turn_group(group - 1)
                        if group == GROUPS - 1:
                            turn_group(group)

            def body(it):
                for k in range(UNROLL):
                    pe_batch(it, k)

            rounds(pe, body)
            pe_batch(ROUNDS, 0)
            pe_batch(ROUNDS, 1)


_INS = ["L0_attn_x", "L0_attn_Wq", "L0_attn_bq", "L0_attn_Wk", "L0_attn_bk", "L0_attn_Wv", "L0_attn_bv",
        "L0_attn_Wo", "L0_attn_bo", "L0_ffn_weight", "L0_ffn_bias"]


def constant_tables():
    import numpy as np

    half = P // 2
    steps = np.arange(half, dtype=np.float32) / np.float32(half)
    frequency = np.float32(1.0) / np.power(np.float32(10000.0), steps, dtype=np.float32)
    angle = np.arange(SEQ, dtype=np.float32)[None, :] * frequency[:, None]
    t = np.zeros((P, T_COLS), np.float32)
    t[:, T_ID:T_ID + P] = np.eye(P, dtype=np.float32)
    t[:, T_COS:T_COS + SEQ] = np.tile(np.cos(angle, dtype=np.float32), (2, 1))
    t[:, T_SIN:T_SIN + 2 * SEQ] = np.tile(np.sin(angle, dtype=np.float32), (2, 2))
    t[:, T_SIN:T_SIN + SEQ] *= np.float32(-1.0)
    t[0::HEAD // 2, T_FLAG] = 1.0
    return t


def kernel(**inputs):
    import numpy as np
    from concourse import bacc
    from concourse.bass_utils import run_bass_kernel_spmd

    nc = bacc.Bacc("TRN2", target_bir_lowering=False, num_devices=1)
    arrays = {"tables": constant_tables()}
    args = [nc.dram_tensor("tables", (P, T_COLS), F32, kind="ExternalInput").ap()]
    for name in _INS:
        a = np.ascontiguousarray(inputs[name])
        arrays[f"in_{name}"] = a
        args.append(nc.dram_tensor(f"in_{name}", a.shape, mybir.dt.from_np(a.dtype), kind="ExternalInput").ap())
    out = nc.dram_tensor("out", (BATCH, SEQ, P), F32, kind="ExternalOutput").ap()
    attention_and_ffn(nc, *args, out)
    r = run_bass_kernel_spmd(nc, [arrays], core_ids=[0])
    return r.results[0]["out"]
```

```python
from contextlib import ExitStack

import concourse.bass as bass
from concourse import mybir

ALU = mybir.AluOpType
ACT = mybir.ActivationFunctionType
AX = mybir.AxisListType
F32 = mybir.dt.float32
F16 = mybir.dt.float16
BF16 = mybir.dt.bfloat16
I32 = mybir.dt.int32

P = 128
BATCH, SEQ, HEADS = 32, 256, 16
HEAD = P // HEADS
TILES = BATCH * SEQ // P
QUADS = HEADS // 4
SCALE = HEAD ** -0.5
EPS = 1e-5
FP8_MAX = 448.0
MAGIC = 1.5 * 2.0 ** 20
TINY = 2.0 ** -6
EXPONENT = 0x7F800000
LEAD = 5
UNROLL = 4
ROUNDS = BATCH // UNROLL
GROUP = 8
GROUPS = TILES // GROUP
GROUP_BUFS = 4
DVE_TILES, ACT_TILES = 2, 3
T_ID, T_COS, T_SIN, T_FLAG = 0, P, P + SEQ, P + 3 * SEQ
T_COLS = T_FLAG + 1

EVEN = {1: ("turn_heads", -2), 2: ("out", -2), 4: ("turn_maxima", 1), 5: ("turn_values", -1), 6: ("k", 4)}
ODD = {1: ("turn_heads", -2), 2: ("out", -2), 3: ("v", 1), 4: ("turn_maxima", 1), 5: ("turn_values", -1),
       6: ("q", 5)}

NORM_GROUPS = {(-4, 1): 2, (-4, 3): 3, (-4, 5): 4, (-4, 6): 5, (-4, 7): 6, (-3, 0): 7}
TURN_GROUPS = {(-4, 1): 1, (-4, 3): 2, (-4, 5): 3, (-4, 6): 4, (-4, 7): 5, (-3, 0): 6, (-2, 4): 7}
LARGEST_OF_GROUPS = {(-4, 1): 1, (-4, 3): 2, (-4, 5): 3, (-4, 6): 4, (-4, 7): 5, (-3, 0): 6, (-2, 6): 7}

FIRST_JOBS = {(-4, 3): ("q", 0), (-4, 5): ("k", 0), (-2, 5): ("q", 2), (-2, 6): ("k", 2), (-1, 0): ("v", 0),
              (-1, 4): ("turn_maxima", 0), (-1, 6): ("q", 4), (-1, 7): ("weight8", 0)}


def job_at(n, k, s):
    if n is not None and n < 0:
        name, j = FIRST_JOBS.get((n, s), (None, 0))
        return name, j - n
    return (ODD if k % 2 else EVEN).get(s, (None, 0))


def plan_side_jobs():
    at = {}
    for n in range(-4, BATCH + 2):
        for s in range(8):
            name, ahead = job_at(n, n, s)
            if name and 0 <= n + ahead < BATCH:
                at[name, n + ahead] = len(at)
    return at


def attention_and_ffn(nc, tables, x, wq, bq, wk, bk, wv, bv, wo, bo, wf, bf, out):
    side_at = plan_side_jobs()
    per_round = len(EVEN) * 2 + len(ODD) * 2

    def exists(it, k):
        return not isinstance(it, int) or 0 <= UNROLL * it + k < BATCH

    def batch(it, k):
        return it * UNROLL + k

    def job(it, k, s):
        return job_at(UNROLL * it + k if isinstance(it, int) else None, k, s)

    def earlier(k, s, slots):
        return (k, s - slots) if s >= slots else (k - 1, s - slots + 8)

    def lead_in(it):
        return isinstance(it, int) and it < 0

    def group_at(groups, it, k, s):
        return groups.get((UNROLL * it + k, s)) if lead_in(it) else None

    def side(name, it, k):
        if isinstance(it, int):
            return side_at.get((name, UNROLL * it + k), -1) + 1
        first = side_at[name, UNROLL + k]
        for r in range(1, ROUNDS - 2):
            assert side_at[name, UNROLL * r + k] == first + per_round * (r - 1)
        return it * per_round + (first - per_round + 1)

    def due(count):
        return not isinstance(count, int) or count > 0

    def pass_wait(engine, semaphore):
        engine.sem_inc(semaphore, 1)

    def rounds(engine, body):
        body(-1)
        body(0)
        with engine.Fori(1, ROUNDS - 2) as it:
            body(it)
        body(ROUNDS - 2)
        body(ROUNDS - 1)

    with ExitStack() as ctx:
        def sbuf(name, shape, dt):
            return ctx.enter_context(nc.sbuf_tensor(name, shape, dt))

        def psum(name, shape, dt):
            return ctx.enter_context(nc.psum_tensor(name, shape, dt))

        def sem(name):
            return ctx.enter_context(nc.semaphore(name))

        scratch = [[nc.dram_tensor(f"scratch_{n}{r}", [P, 2, 4, SEQ], F16, kind="Internal").ap()
                    for r in range(2)] for n in "qk"]

        table = sbuf("table", [P, T_COLS], F32)
        ident = table[:, T_ID:T_ID + P]
        ident16 = sbuf("ident16", [P, P], F16)
        identb = sbuf("identb", [P, P], BF16)
        raw = sbuf("raw", [P, 5, P], F32)
        wo_order = sbuf("wo_order", [P, P], F32)
        wqT = sbuf("wqT", [P, P], F32)
        wkT = sbuf("wkT", [P, P], F32)
        wvT = sbuf("wvT", [P, P], F32)
        woT = sbuf("woT", [P, P], F32)
        w8 = sbuf("w8", [P, P], BF16)
        w8T = sbuf("w8T", [P, P], BF16)
        bias_rows = sbuf("bias_rows", [3, 4, P], F32)
        bias_cols = sbuf("bias_cols", [P, 3, 3], F32)
        bv_wide = sbuf("bv_wide", [P, P], F32)
        bo_rows = sbuf("bo_rows", [P, P], F32)
        bf_rows = sbuf("bf_rows", [P, P], F32)
        small = sbuf("small", [P, 16], F32)
        quant_w = sbuf("quant_w", [P, 4, P], F32)
        fill = sbuf("fill", [P, 2, 2 * SEQ], F16)

        xg = sbuf("xg", [P, GROUP_BUFS, GROUP, P], F32)
        xn = sbuf("xn", [P, 2, GROUP, P], F32)
        stats = sbuf("stats", [P, 2, GROUP, 6], F32)
        moments = sbuf("moments", [P, 2, GROUP, 2], F32)
        spread = sbuf("spread", [P, 2, GROUP], F32)
        root = sbuf("root", [P, 2, GROUP], F32)
        rstd = sbuf("rstd", [P, 2, GROUP], F32)
        newton = sbuf("newton", [P, GROUP], F32)
        minus_mean = sbuf("minus_mean", [P, 2, GROUP], F32)
        centred = sbuf("centred", [P, ACT_TILES, P], F32)
        largest = sbuf("largest", [P, GROUPS], F32)
        xnT = sbuf("xnT", [P, BATCH * SEQ], F32)

        xc = sbuf("xc", [P, 2, 2 * SEQ], F32)
        turned = sbuf("turned", [P, 2, 3, 2 * SEQ], F32)
        rotated = sbuf("rotated", [P, 2 * SEQ], F32)
        parts = sbuf("parts", [P, 2, 2, 2, SEQ], F16)
        q_stack = sbuf("q_stack", [P, UNROLL, QUADS, SEQ], F16)
        k_stack = sbuf("k_stack", [P, UNROLL, HEADS, SEQ], F16)
        maxima = sbuf("maxima", [P, 2, 2, HEADS], F16)
        max_rows = sbuf("max_rows", [HEADS, 2, SEQ], F16)
        probs = sbuf("probs", [P, 8, 2 * SEQ], F32)
        v_pad = sbuf("v_pad", [P, UNROLL, 2, HEADS, 32], F32)
        valuesT = sbuf("valuesT", [P, 2 * SEQ], F32)
        inverse = sbuf("inverse", [P, 32], F32)
        heads = sbuf("heads", [P, SEQ], F32)
        headsT = sbuf("headsT", [P, SEQ], F32)
        x8_scaled = sbuf("x8_scaled", [P, SEQ], F32)
        x8_clipped = sbuf("x8_clipped", [P, SEQ], F32)
        x8_magic = sbuf("x8_magic", [P, 2, SEQ], F32)
        x8_sum = sbuf("x8_sum", [P, SEQ], F32)
        x8 = sbuf("x8", [P, 2, SEQ], BF16)
        x_rows = sbuf("x_rows", [P, 2, 2, P], F32)
        x_bias = sbuf("x_bias", [P, 2, P], F32)
        ffn = sbuf("ffn", [P, 2, P], BF16)
        attn = sbuf("attn", [P, 2, P], F32)
        result = sbuf("result", [P, 2, 2, P], F32)

        ps_rows = [psum(f"ps_rows{r}", [P, 4, SEQ], F32) for r in range(2)]
        ps_cols = [psum(f"ps_cols{r}", [P, 2 * SEQ], F32) for r in range(2)]
        ps_values = psum("ps_values", [P, 2 * SEQ], F32)
        ps_side = psum("ps_side", [P, 2 * SEQ], F32)
        ps_side16 = ps_side[:].bitcast(F16)
        ps_sideb = ps_side[:].bitcast(BF16)

        setup_loaded = sem("setup_loaded")
        dve_step = sem("dve_step")
        stacks_cleared = sem("stacks_cleared")
        weight_largest = sem("weight_largest")
        biases_ready = sem("biases_ready")
        bias_cols_ready = sem("bias_cols_ready")
        stats_ready = sem("stats_ready")
        pool_filled = sem("pool_filled")
        biases_turned = sem("biases_turned")
        weights_turned = sem("weights_turned")
        weights_ready = sem("weights_ready")
        fill_stored = sem("fill_stored")
        weight_reduced = sem("weight_reduced")
        weight_step = sem("weight_step")
        scale_step = sem("scale_step")
        rows_loaded = [sem(f"rows_loaded{r}") for r in range(GROUP_BUFS)]
        variance_ready = sem("variance_ready")
        root_ready = sem("root_ready")
        rstd_ready = sem("rstd_ready")
        normalised = sem("normalised")
        pool_normalised = sem("pool_normalised")
        act_normalised = sem("act_normalised")
        act_centred = sem("act_centred")
        group_largest = sem("group_largest")
        wide_ready = sem("wide_ready")
        group_turned = sem("group_turned")
        group_copied = sem("group_copied")
        largest_ready = sem("largest_ready")
        largest_reduced = sem("largest_reduced")

        sp_passed, pool_passed = sem("sp_passed"), sem("pool_passed")

        xc_loaded = [sem(f"xc_loaded{r}") for r in range(2)]
        side_written = sem("side_written")
        side_read = sem("side_read")
        products_ready = sem("products_ready")
        pool_rotated = sem("pool_rotated")
        high_cut = sem("high_cut")
        low_cut = sem("low_cut")
        parts_stored = [sem(f"parts_stored{c}") for c in "qk"]
        stack_loaded = [sem(f"stack_loaded{r}") for r in range(UNROLL)]
        shift_loaded = [[sem(f"shift_loaded{t}{r}") for r in range(2)] for t in range(QUADS)]
        rows_scored = sem("rows_scored")
        rows_reduced = sem("rows_reduced")
        cols_scored = sem("cols_scored")
        probs_ready = sem("probs_ready")
        values_summed = sem("values_summed")
        values_copied = sem("values_copied")
        sums_inverted = sem("sums_inverted")
        x8_scaled_ready = sem("x8_scaled_ready")
        x8_exponent_ready = sem("x8_exponent_ready")
        x8_clipped_ready = sem("x8_clipped_ready")
        x8_magic_ready = sem("x8_magic_ready")
        x8_sum_ready = sem("x8_sum_ready")
        x8_ready = sem("x8_ready")
        x_loaded = [sem(f"x_loaded{r}") for r in range(2)]
        x_bias_ready = sem("x_bias_ready")
        result_ready = sem("result_ready")
        stored = [sem(f"stored{r}") for r in range(2)]

        amax_w, amax_w_all, scale_w, inv_w = (small[:, i:i + 1] for i in range(4))
        amax_x, amax_x_all, scale_x, inv_x = (small[:, i:i + 1] for i in range(4, 8))
        unscale = small[:, 8:9]
        SETUP_LOADS = 11

        def even_first(ap):
            return ap.rearrange("p (i two) -> p two i", two=2)

        def turned_rows(r, half):
            return ps_cols[half][:] if r else ps_rows[1][:, 2 * half:2 * half + 2].rearrange("p a b -> p (a b)")

        block = ctx.enter_context(nc.Block())

        @block.sync
        def _(sp):
            sp.dma_start(table[:], tables).then_inc(setup_loaded, 16)
            for i, w in enumerate((wq, wk, wv, wo, wf)):
                sp.dma_start(raw[:, i, :], w).then_inc(setup_loaded, 16)
            for i, b in enumerate((bq, bk, bv)):
                sp.dma_start(bias_rows[i:i + 1, 0, :], b.rearrange("(one f) -> one f", one=1))\
                  .then_inc(setup_loaded, 16)
            sp.dma_start(bo_rows[:], bo.partition_broadcast(P)).then_inc(setup_loaded, 16)
            sp.dma_start(bf_rows[:], bf.partition_broadcast(P)).then_inc(setup_loaded, 16)

            sp.wait_ge(pool_filled, 5)
            for c in range(2):
                for r in range(2):
                    sp.dma_start(scratch[c][r][:, :, 3, :], fill[:, c, :].rearrange("p (two w) -> p two w", two=2))\
                      .then_inc(fill_stored, 16)
            sp.wait_ge(fill_stored, 64)

            def load_xc(it, k):
                if exists(it, k):
                    r = (k // 2) % 2
                    sp.wait_ge(group_copied, it + k // 4 + 1)
                    pass_wait(sp, sp_passed)
                    if due(count := side("v", it, k - 4)):
                        sp.wait_ge(side_written, count)
                        pass_wait(sp, sp_passed)
                    src = xnT[:, bass.ds(batch(it, k) * SEQ, 2 * SEQ)]
                    sp.dma_start(xc[:, r, :], src).then_inc(xc_loaded[r], 16)

            def store_parts(c, it, k):
                if not exists(it, k):
                    return
                r = (k // 2) % 2
                pair = it * 2 + k // 2
                for b in range(2):
                    if due(count := (it + (k - 4) // 4 + 1) * 80):
                        sp.wait_ge(stack_loaded[(k + b) % UNROLL], count)
                        pass_wait(sp, sp_passed)
                sp.wait_ge(low_cut, pair * 2 + c + 1)
                pass_wait(sp, sp_passed)
                one, two = (slice(0, 1), slice(1, 3)) if c == 0 else (slice(2, 3), slice(0, 2))
                sp.dma_start(scratch[c][r][:, :, one], parts[:, c, :, 0:1]).then_inc(parts_stored[c], 16)
                sp.dma_start(scratch[c][r][:, :, two], parts[:, c]).then_inc(parts_stored[c], 16)

            def load_stacks(it, k):
                if not exists(it, k):
                    return
                r, b, buf = (k // 2) % 2, k % 2, k % UNROLL
                pair = it * 2 + k // 2
                if due(count := (batch(it, k) - 3) * HEADS):
                    sp.wait_ge(cols_scored, count)
                    pass_wait(sp, sp_passed)
                sp.wait_ge(parts_stored[0], pair * 32 + 32)
                pass_wait(sp, sp_passed)
                src = scratch[0][r].rearrange("(b t f) two c w -> b (f two c) t w", b=2, t=QUADS)
                sp.dma_start(q_stack[:, buf], src[b]).then_inc(stack_loaded[buf], 16)
                sp.wait_ge(parts_stored[1], pair * 32 + 32)
                pass_wait(sp, sp_passed)
                src = scratch[1][r].rearrange("(b t f) two c w -> b (f two c) t w", b=2, t=QUADS)
                sp.wait_ge(stacks_cleared, 1)
                for j in range(4):
                    rows = slice(32 * j, 32 * j + 32)
                    sp.dma_start(k_stack[rows, buf, j:HEADS:4, :], src[b, rows])\
                      .then_inc(stack_loaded[buf], 16)

            def load_shift(it, k):
                if not exists(it, k):
                    return
                buf = k % UNROLL
                sp.wait_ge(side_read, side("turn_maxima", it, k))
                pass_wait(sp, sp_passed)
                for t in range(QUADS):
                    sp.dma_start(q_stack[3:P:32, buf, t, :], max_rows[4 * t:4 * t + 4, k % 2, :])\
                      .then_inc(shift_loaded[t][k % 2], 16)

            def store_result(it, k):
                if exists(it, k):
                    sp.wait_ge(result_ready, batch(it, k) + 1)
                    pass_wait(sp, sp_passed)
                    dst = out[bass.ds(batch(it, k), 1)].rearrange("o (t p) d -> p (o t) d", p=P)
                    sp.dma_start(dst, result[:, k % 2]).then_inc(stored[k % 2], 16)

            def load_x(it, k):
                if exists(it, k):
                    if due(count := batch(it, k) - 1):
                        sp.wait_ge(x_bias_ready, count)
                        pass_wait(sp, sp_passed)
                    src = x[bass.ds(batch(it, k), 1)].rearrange("o (t p) d -> p (o t) d", p=P)
                    sp.dma_start(x_rows[:, k % 2], src).then_inc(x_loaded[k % 2], 16)

            def body(it):
                for k in range(0, UNROLL, 2):
                    if not (lead_in(it) and k == 2):
                        load_xc(it, k + 4)
                    if lead_in(it) and k == 0:
                        load_xc(it, k + 6)
                    store_parts(1, it, k + 2)
                    load_shift(it, k)
                    load_x(it, k - 1)
                    store_result(it, k - 3)
                    load_stacks(it, k + 2)
                    load_stacks(it, k + 3)
                    store_parts(0, it, k + 4)
                    load_shift(it, k + 1)
                    load_x(it, k)
                    store_result(it, k - 2)

            rounds(sp, body)
            load_x(ROUNDS, -1)
            for k in (-3, -2, -1):
                store_result(ROUNDS, k)
            for r in range(2):
                sp.wait_ge(stored[r], BATCH // 2 * 16)

        @block.gpsimd
        def _(pool):
            g = nc.gpsimd
            g.memset(k_stack[:, 2:4].bitcast(F32), 0.0).then_inc(pool_filled, 1)
            g.memset(v_pad[:], 0.0).then_inc(pool_filled, 1)
            pool.wait_ge(pool_filled, 2)
            quads = v_pad[:].rearrange("p b kt (g e j) c -> p (b kt g) e j c", e=2, j=4)
            for e in range(2):
                g.memset(quads[:, :, e, :, 16 * e + 8], 1.0).then_inc(pool_filled, 1)

            def normalise(group):
                r = group % 2
                pool.wait_ge(rstd_ready, group + 1)
                if due(count := group - 1):
                    pool.wait_ge(group_turned, count)
                if due(count := group - 1):
                    pool.wait_ge(group_largest, count)
                for i in range(DVE_TILES + ACT_TILES, GROUP):
                    ins = g.tensor_scalar(xn[:, r, i, :], xg[:, group % GROUP_BUFS, i, :], moments[:, r, i, 0:1],
                                          rstd[:, r, i:i + 1], ALU.subtract, ALU.mult)
                ins.then_inc(pool_normalised, 1)

            normalise(0)
            pool.wait_ge(setup_loaded, 16 * SETUP_LOADS)
            g.memset(fill[:, 0, :], 0.0)
            g.memset(fill[:, 1, SEQ:2 * SEQ], 0.0)
            g.tensor_scalar(fill[:, 1, 0:SEQ], table[:, T_FLAG:T_FLAG + 1].to_broadcast([P, SEQ]), 1.0, None,
                            ALU.mult).then_inc(pool_filled, 1)
            pool.wait_ge(weight_largest, 1)
            g.partition_all_reduce(amax_w_all, amax_w, P, bass.bass_isa.ReduceOp.absmax).then_inc(weight_reduced, 1)
            for group in (1, 2, 3):
                normalise(group)

            def cut(c, it, k):
                if not exists(it, k):
                    return
                done = (it * 2 + k // 2) * 2 + c
                pool.wait_ge(products_ready, done + 1)
                if due(count := done):
                    pool.wait_ge(low_cut, count)
                g.tensor_tensor(rotated[:], turned[:, c, 1, :], turned[:, c, 2, :], ALU.add).then_inc(pool_rotated, 1)
                pool.wait_ge(pool_rotated, done + 1)
                if due(count := (it * 2 + k // 2) * 32):
                    pool.wait_ge(parts_stored[c], count)
                pass_wait(pool, pool_passed)
                whole = rotated[:].rearrange("p (two w) -> p two w", two=2)
                g.tensor_scalar(parts[:, c, :, 0], whole, 1.0, None, ALU.mult).then_inc(high_cut, 1)
                pool.wait_ge(high_cut, done + 1)
                g.tensor_tensor(parts[:, c, :, 1], whole, parts[:, c, :, 0], ALU.subtract).then_inc(low_cut, 1)

            def add_bias(it, k):
                if exists(it, k):
                    if isinstance(it, int) and batch(it, k) == 0:
                        pool.wait_ge(side_read, side("weight8", 0, 0))
                    pool.wait_ge(x_loaded[k % 2], (it * 2 + k // 2 + 1) * 16)
                    if due(count := side("out", it, k - 1)):
                        pool.wait_ge(side_read, count)
                    bias = bo_rows[:].rearrange("p (one d) -> p one d", one=1).to_broadcast([P, 2, P])
                    g.tensor_tensor(x_bias[:], x_rows[:, k % 2], bias, ALU.add).then_inc(x_bias_ready, 1)

            def quantise(it, k):
                if not exists(it, k):
                    return
                n = batch(it, k) + 1
                if due(count := n - 1):
                    pool.wait_ge(x8_ready, count)
                pool.wait_ge(x8_exponent_ready, n)
                pass_wait(pool, pool_passed)
                g.tensor_scalar(x8_magic[:, 1, :], x8_magic[:, 0, :], TINY, MAGIC, ALU.max, ALU.mult)\
                 .then_inc(x8_magic_ready, 1)
                g.tensor_scalar(x8_clipped[:], x8_scaled[:], -FP8_MAX, None, ALU.max).then_inc(x8_clipped_ready, 1)
                pool.wait_ge(x8_magic_ready, n)
                pool.wait_ge(x8_clipped_ready, n)
                g.tensor_tensor(x8_sum[:], x8_clipped[:], x8_magic[:, 1, :], ALU.add).then_inc(x8_sum_ready, 1)
                pool.wait_ge(x8_sum_ready, n)
                if due(count := side("out", it, k - 2)):
                    pool.wait_ge(side_written, count)
                g.tensor_tensor(x8[:, k % 2, :], x8_sum[:], x8_magic[:, 1, :], ALU.subtract).then_inc(x8_ready, 1)

            def finish(it, k):
                if exists(it, k):
                    pool.wait_ge(side_read, side("out", it, k))
                    if due(count := (it * 2 + k // 2) * 16):
                        pool.wait_ge(stored[k % 2], count)
                    g.tensor_tensor(result[:, k % 2], attn[:], ffn[:], ALU.add).then_inc(result_ready, 1)

            def body(it):
                for k in range(UNROLL):
                    if lead_in(it) and k == 1:
                        normalise(4)
                    if lead_in(it) and k == 2:
                        for group in (5, 6, 7):
                            normalise(group)
                    if lead_in(it) and k == 3:
                        pool.wait_ge(largest_ready, 1)
                        g.partition_all_reduce(amax_x_all, amax_x, P, bass.bass_isa.ReduceOp.absmax)\
                         .then_inc(largest_reduced, 1)
                    cut(k % 2, it, k + 4 - k % 2)
                    finish(it, k - 2)
                    add_bias(it, k - 1)
                    quantise(it, k)

            rounds(pool, body)
            finish(ROUNDS, -2)
            add_bias(ROUNDS, -1)
            finish(ROUNDS, -1)

        @block.scalar
        def _(act):
            x_tiles = x.rearrange("b (t p) d -> (b t) p d", p=P)

            def load_group(group):
                if due(count := group - GROUP_BUFS + 1):
                    act.wait_ge(normalised, count)
                if due(count := group - GROUP_BUFS + 1):
                    act.wait_ge(pool_normalised, count)
                if due(count := group - GROUP_BUFS + 1):
                    act.wait_ge(act_normalised, count)
                act.dma_start(xg[:, group % GROUP_BUFS],
                              x_tiles[group * GROUP:(group + 1) * GROUP].rearrange("t p d -> p t d"))\
                   .then_inc(rows_loaded[group % GROUP_BUFS], 16)

            def take_root(group):
                r = group % 2
                act.wait_ge(variance_ready, group + 1)
                nc.scalar.activation(root[:, r, :], spread[:, r, :], ACT.Sqrt).then_inc(root_ready, 1)

            def normalise(group):
                r = group % 2
                if due(count := group):
                    act.wait_ge(act_normalised, count)
                for i in range(ACT_TILES):
                    ins = nc.scalar.activation(centred[:, i, :], xg[:, group % GROUP_BUFS, DVE_TILES + i, :],
                                               ACT.Identity, bias=minus_mean[:, r, DVE_TILES + i:DVE_TILES + i + 1])
                ins.then_inc(act_centred, 1)
                act.wait_ge(act_centred, group + 1)
                act.wait_ge(rstd_ready, group + 1)
                if due(count := group - 1):
                    act.wait_ge(group_turned, count)
                if due(count := group - 1):
                    act.wait_ge(group_largest, count)
                for i in range(ACT_TILES):
                    ins = nc.scalar.activation(xn[:, r, DVE_TILES + i, :], centred[:, i, :], ACT.Copy,
                                               scale=rstd[:, r, DVE_TILES + i:DVE_TILES + i + 1])
                ins.then_inc(act_normalised, 1)

            def copy_group(group):
                r = group % 2
                act.wait_ge(group_turned, group + 1)
                for i in range(2):
                    to = (group * 2 + i) * 2 * SEQ
                    ins = nc.scalar.copy(xnT[:, to:to + 2 * SEQ], turned_rows(r, i))
                ins.then_inc(group_copied, 1)

            for group in range(GROUP_BUFS):
                load_group(group)
            take_root(0)
            normalise(0)

            act.wait_ge(weights_turned, 1)
            turned_weights = [ps_side[:, i * P:(i + 1) * P] for i in range(4)]
            for w, p in ((wqT, turned_weights[0]), (wkT, turned_weights[1])):
                nc.scalar.copy(w[:].rearrange("p (two i) -> p two i", two=2), even_first(p))
            nc.scalar.copy(wvT[:], turned_weights[2])
            nc.scalar.copy(woT[:], turned_weights[3]).then_inc(weights_ready, 1)
            take_root(1)
            normalise(1)
            copy_group(0)

            def exponential(it, k, h):
                if not exists(it, k):
                    return
                done = batch(it, k) * HEADS + h
                if h % 4 == 0:
                    if due(count := batch(it, k) * QUADS + h // 4 - 1):
                        act.wait_ge(values_summed, count)
                act.wait_ge(cols_scored, done + 1)
                nc.scalar.activation(probs[:, h % 8, :], ps_cols[h % 2][:], ACT.Exp, scale=SCALE)\
                  .then_inc(probs_ready, 1)

            def side_job(it, k, s):
                name, ahead = job(it, k, s)
                j = k + ahead
                if name not in ("q", "k", "v", "turn_maxima", "turn_heads") or not exists(it, j):
                    return
                act.wait_ge(side_written, side(name, it, j))
                if name in ("q", "k"):
                    c = int(name == "k")
                    if due(count := (it * 2 + j // 2) * 2 + c - 1):
                        act.wait_ge(pool_rotated, count)
                    for two in range(2):
                        cols = slice(two * SEQ, (two + 1) * SEQ)
                        ins = nc.scalar.activation(turned[:, c, 0, cols], ps_side[:, cols], ACT.Identity,
                                                   bias=bias_cols[:, two, c:c + 1])
                elif name == "turn_maxima":
                    ins = nc.scalar.copy(max_rows[:, j % 2, :], ps_side16[0:HEADS, 0:SEQ])
                elif name == "turn_heads":
                    if due(count := side("out", it, j - 1)):
                        act.wait_ge(side_written, count)
                    ins = nc.scalar.copy(headsT[:], ps_side[:, 0:SEQ])
                else:
                    if due(count := (batch(it, j) - 2) * QUADS):
                        act.wait_ge(values_summed, count)
                    act.wait_ge(pool_filled, 5)
                    for b in range(2):
                        cols = slice(b * SEQ, (b + 1) * SEQ)
                        src = ps_side[:, cols].rearrange("p (a e j d) -> p a e j d", e=2, j=4, d=HEAD)
                        dst = v_pad[:, (j + b) % UNROLL].rearrange("p kt (g e j) c -> p (kt g) e j c", e=2, j=4)
                        for e in range(2):
                            ins = nc.scalar.copy(dst[:, :, e, :, 16 * e:16 * e + HEAD], src[:, :, e])
                ins.then_inc(side_read, 1)

            def copy_values(it, k):
                if exists(it, k):
                    act.wait_ge(values_summed, batch(it, k) * QUADS + QUADS)
                    if due(count := side("turn_values", it, k - 1)):
                        act.wait_ge(side_written, count)
                    nc.scalar.copy(valuesT[:], ps_values[:]).then_inc(values_copied, 1)

            def act_batch(it, k):
                for s in range(8):
                    exponential(it, k, 2 * s)
                    exponential(it, k, 2 * s + 1)
                    if s == 1:
                        copy_values(it, k - 1)
                    if group := group_at(NORM_GROUPS, it, k, s):
                        take_root(group)
                        if GROUP_BUFS <= group + 2 < GROUPS:
                            load_group(group + 2)
                        normalise(group)
                    side_job(it, k, s)
                    if group := group_at(TURN_GROUPS, it, k, s):
                        copy_group(group)

            def body(it):
                for k in range(UNROLL):
                    act_batch(it, k)

            rounds(act, body)
            act_batch(ROUNDS, 0)
            act_batch(ROUNDS, 1)

        @block.vector
        def _(dve):
            v = nc.vector
            steps = [0]

            def step(ins):
                steps[0] += 1
                ins.then_inc(dve_step, 1)
                dve.wait_ge(dve_step, steps[0])

            def begin(ins):
                steps[0] += 1
                ins.then_inc(dve_step, 1)

            def take_stats(group, tiles):
                for i in tiles:
                    v.bn_stats(stats[:, group % 2, i, :], xg[:, group % GROUP_BUFS, i, :]).then_inc(stats_ready, 1)

            def norm_group(group):
                r = group % 2

                def fill_in(*tiles):
                    if group + 1 < GROUPS:
                        if 0 in tiles:
                            dve.wait_ge(rows_loaded[(group + 1) % GROUP_BUFS], ((group + 1) // GROUP_BUFS + 1) * 16)
                        take_stats(group + 1, tiles)

                if due(count := group - 1):
                    dve.wait_ge(pool_normalised, count)
                if due(count := group - 1):
                    dve.wait_ge(act_normalised, count)
                dve.wait_ge(stats_ready, group * GROUP + GROUP)
                for i in range(GROUP):
                    ins = v.bn_aggr(moments[:, r, i, :], stats[:, r, i, :])
                step(ins)
                v.tensor_scalar(minus_mean[:, r, :], moments[:, r, :, 0], -1.0, None, ALU.mult)
                v.tensor_scalar(spread[:, r, :], moments[:, r, :, 1], EPS, None, ALU.add).then_inc(variance_ready, 1)
                fill_in(0, 1, 2, 3)
                dve.wait_ge(root_ready, group + 1)
                begin(v.reciprocal(rstd[:, r, :], root[:, r, :]))
                fill_in(4)
                dve.wait_ge(dve_step, steps[0])
                begin(v.tensor_tensor(newton[:], rstd[:, r, :], rstd[:, r, :], ALU.mult))
                fill_in(5)
                dve.wait_ge(dve_step, steps[0])
                begin(v.tensor_tensor(newton[:], newton[:], spread[:, r, :], ALU.mult))
                fill_in(6)
                dve.wait_ge(dve_step, steps[0])
                begin(v.tensor_scalar(newton[:], newton[:], -0.5, 1.5, ALU.mult, ALU.add))
                dve.wait_ge(dve_step, steps[0])
                v.tensor_tensor(rstd[:, r, :], rstd[:, r, :], newton[:], ALU.mult).then_inc(rstd_ready, 1)
                fill_in(7)
                dve.wait_ge(rstd_ready, group + 1)
                if due(count := group - 1):
                    dve.wait_ge(group_turned, count)
                for i in range(DVE_TILES):
                    ins = v.tensor_scalar(xn[:, r, i, :], xg[:, group % GROUP_BUFS, i, :], moments[:, r, i, 0:1],
                                          rstd[:, r, i:i + 1], ALU.subtract, ALU.mult)
                ins.then_inc(normalised, 1)

            def group_max(group):
                dve.wait_ge(normalised, group + 1)
                dve.wait_ge(pool_normalised, group + 1)
                dve.wait_ge(act_normalised, group + 1)
                v.tensor_reduce(largest[:, group:group + 1], xn[:, group % 2].rearrange("p a b -> p (a b)"), AX.X,
                                ALU.max, apply_absolute_value=True).then_inc(group_largest, 1)

            v.memset(k_stack[:, 0:2].bitcast(F32), 0.0).then_inc(stacks_cleared, 1)
            dve.wait_ge(rows_loaded[0], 16)
            take_stats(0, range(GROUP))
            norm_group(0)

            dve.wait_ge(setup_loaded, 16 * SETUP_LOADS)
            v.tensor_reduce(amax_w, raw[:, 4, :], AX.X, ALU.max, apply_absolute_value=True)\
             .then_inc(weight_largest, 1)
            v.tensor_copy(ident16[:], ident)
            v.tensor_copy(identb[:], ident)
            def reorder(dst, src):
                for g in range(2):
                    to = dst[:, 64 * g:64 * g + 64].rearrange("p (j e d) -> p j e d", e=2, j=4)
                    v.tensor_copy(to, src[:, 64 * g:64 * g + 64].rearrange("p (e j d) -> p j e d", e=2, j=4))

            reorder(wo_order[:], raw[:, 3, :])
            reorder(bias_rows[:, 3, :], bias_rows[:, 0, :])
            for b in range(2):
                ins = v.tensor_copy(bias_rows[:, 1:3, b * P // 2:(b + 1) * P // 2], even_first(bias_rows[:, 0, :]))
            ins.then_inc(biases_ready, 1)
            dve.wait_ge(biases_turned, 1)
            v.tensor_copy(bias_cols[:], ps_side[:, 0:9].rearrange("p (a b) -> p a b", a=3))\
             .then_inc(bias_cols_ready, 1)
            dve.wait_ge(bias_cols_ready, 1)
            v.tensor_copy(bv_wide[:], bias_cols[:, 2, 2:3].to_broadcast([P, P])).then_inc(wide_ready, 1)
            norm_group(1)
            group_max(0)

            def find_scale(i, amax_all, scale, inverse_scale):
                if i == 0:
                    return v.tensor_scalar(scale, amax_all, 1e-12, None, ALU.max)
                if i == 1:
                    return v.reciprocal(inverse_scale, scale)
                if i == 2:
                    return v.tensor_scalar(scale, inverse_scale, FP8_MAX, FP8_MAX, ALU.mult, ALU.min)
                return v.reciprocal(inverse_scale, scale)

            def quantise_weight(i):
                if i == 0:
                    dve.wait_ge(weight_reduced, 1)
                else:
                    dve.wait_ge(weight_step, i)
                y, m, t, z = (quant_w[:, column, :] for column in range(4))
                if i < 4:
                    ins = find_scale(i, amax_w_all, scale_w, inv_w)
                elif i == 4:
                    ins = v.tensor_scalar(y, raw[:, 4, :], scale_w, FP8_MAX, ALU.mult, ALU.min)
                elif i == 5:
                    ins = v.tensor_scalar(z, y, -FP8_MAX, None, ALU.max)
                elif i == 6:
                    ins = v.tensor_scalar(m.bitcast(I32), z.bitcast(I32), EXPONENT, None, ALU.bitwise_and)
                elif i == 7:
                    ins = v.tensor_scalar(t, m, TINY, MAGIC, ALU.max, ALU.mult)
                elif i == 8:
                    ins = v.tensor_tensor(y, z, t, ALU.add)
                else:
                    ins = v.tensor_tensor(w8[:], y, t, ALU.subtract)
                ins.then_inc(weight_step, 1)

            def scale_xn(i):
                if i == 0:
                    dve.wait_ge(largest_reduced, 1)
                else:
                    dve.wait_ge(scale_step, i)
                if i < 4:
                    ins = find_scale(i, amax_x_all, scale_x, inv_x)
                else:
                    ins = v.tensor_tensor(unscale, inv_x, inv_w, ALU.mult)
                ins.then_inc(scale_step, 1)

            def find_largest():
                dve.wait_ge(group_largest, GROUPS)
                v.tensor_reduce(amax_x, largest[:], AX.X, ALU.max).then_inc(largest_ready, 1)

            def row_maxima(it, k, s):
                ka, u = k + 1 + (s + LEAD) // 8, (s + LEAD) % 8
                if not exists(it, ka):
                    return
                done = batch(it, ka) * 8 + u
                if u == 0:
                    if due(count := side("turn_maxima", it, ka - 2)):
                        dve.wait_ge(side_written, count)
                dve.wait_ge(rows_scored, done + 1)
                v.tensor_reduce(maxima[:, ka % 2, u % 2, 4 * (u // 2):4 * (u // 2) + 4], ps_rows[u % 2][:],
                                AX.X, ALU.max, negate=True).then_inc(rows_reduced, 1)

            def side_job(it, k, s):
                name, ahead = job(it, k, s)
                j = k + ahead
                if name not in ("turn_values", "out", "weight8") or not exists(it, j):
                    return
                dve.wait_ge(side_written, side(name, it, j))
                if name == "turn_values":
                    groups = ps_side[:].rearrange("p (h c) -> p h c", c=16)
                    v.reciprocal(inverse[:], groups[:, :, 8]).then_inc(sums_inverted, 1)
                    dve.wait_ge(sums_inverted, batch(it, j) + 1)
                    if due(count := side("turn_heads", it, j - 1)):
                        dve.wait_ge(side_written, count)
                    factor = inverse[:].rearrange("p (h one) -> p h one", one=1).to_broadcast([P, 32, HEAD])
                    ins = v.tensor_tensor(heads[:].rearrange("p (h d) -> p h d", d=HEAD), groups[:, :, 0:HEAD],
                                          factor, ALU.mult)
                elif name == "weight8":
                    v.tensor_copy(w8T[:], ps_sideb[:, 0:P])
                    ins = v.tensor_tensor(bo_rows[:], bo_rows[:], ps_side[:, P:2 * P], ALU.add)
                else:
                    dve.wait_ge(scale_step, 5)
                    if due(count := batch(it, j)):
                        dve.wait_ge(result_ready, count)
                    dve.wait_ge(x_bias_ready, batch(it, j) + 1)
                    bias = bf_rows[:].rearrange("p (one d) -> p one d", one=1).to_broadcast([P, 2, P])
                    both = ps_side[:].rearrange("p (a t d) -> p a t d", a=2, t=2)
                    v.scalar_tensor_tensor(ffn[:], both[:, 1], unscale, bias, ALU.mult, ALU.add)
                    ins = v.tensor_tensor(attn[:], both[:, 0], x_bias[:], ALU.add)
                ins.then_inc(side_read, 1)

            def multiply_waves(it, k, s):
                k, s = earlier(k, s, 1)
                name, ahead = job(it, k, s)
                j = k + ahead
                if name not in ("q", "k") or not exists(it, j):
                    return
                c = int(name == "k")
                dve.wait_ge(side_read, side(name, it, j))
                q = turned[:, c, 0, :].rearrange("p (two w) -> p two w", two=2)
                v.tensor_tensor(turned[:, c, 1, :].rearrange("p (two w) -> p two w", two=2), q[:, ::-1],
                                table[:, T_SIN:T_SIN + 2 * SEQ].rearrange("p (two w) -> p two w", two=2), ALU.mult)
                cos = table[:, T_COS:T_COS + SEQ].rearrange("p (one w) -> p one w", one=1).to_broadcast([P, 2, SEQ])
                v.tensor_tensor(turned[:, c, 2, :].rearrange("p (two w) -> p two w", two=2), q, cos, ALU.mult)\
                 .then_inc(products_ready, 1)

            def scale_x8(it, k):
                if not exists(it, k):
                    return
                dve.wait_ge(group_copied, it + k // 4 + 1)
                if due(count := batch(it, k)):
                    dve.wait_ge(x8_sum_ready, count)
                v.tensor_scalar(x8_scaled[:], xnT[:, bass.ds(batch(it, k) * SEQ, SEQ)], scale_x, FP8_MAX,
                                ALU.mult, ALU.min).then_inc(x8_scaled_ready, 1)
                dve.wait_ge(x8_scaled_ready, batch(it, k) + 1)
                v.tensor_scalar(x8_magic[:, 0, :].bitcast(I32), x8_scaled[:].bitcast(I32), EXPONENT, None,
                                ALU.bitwise_and).then_inc(x8_exponent_ready, 1)

            def dve_batch(it, k):
                for s in range(8):
                    row_maxima(it, k, s)
                    side_job(it, k, s)
                    multiply_waves(it, k, s)
                    if s == 6:
                        scale_x8(it, k)
                    if group := group_at(NORM_GROUPS, it, k, s):
                        norm_group(group)
                    if group := group_at(LARGEST_OF_GROUPS, it, k, s):
                        group_max(group)
                        if group == GROUPS - 1:
                            find_largest()
                    if lead_in(it) and 0 <= (k - 2) * 8 + s - 3 < 10:
                        quantise_weight((k - 2) * 8 + s - 3)
                    if lead_in(it) and k == 3 and 2 <= s < 7:
                        scale_xn(s - 2)

            def body(it):
                for k in range(UNROLL):
                    dve_batch(it, k)

            rounds(dve, body)
            dve_batch(ROUNDS, 0)
            dve_batch(ROUNDS, 1)

        @block.tensor
        def _(pe):
            mm = nc.tensor.matmul
            def turn_group(group):
                r = group % 2
                pe.wait_ge(normalised, group + 1)
                pe.wait_ge(pool_normalised, group + 1)
                pe.wait_ge(act_normalised, group + 1)
                if due(count := group - 1):
                    pe.wait_ge(group_copied, count)
                for i in range(GROUP):
                    ins = nc.tensor.transpose(turned_rows(r, i // 4)[:, i % 4 * P:(i % 4 + 1) * P], xn[:, r, i, :],
                                              ident)
                ins.then_inc(group_turned, 1)

            pe.wait_ge(biases_ready, 1)
            for i in range(3):
                ins = nc.tensor.transpose(ps_side[:, 3 * i:3 * i + 3], bias_rows[:, i + 1, :], ident[0:3, 0:3])
            ins.then_inc(biases_turned, 1)
            pe.wait_ge(bias_cols_ready, 1)
            for i in range(3):
                nc.tensor.transpose(ps_side[:, i * P:(i + 1) * P], raw[:, i, :], ident)
            nc.tensor.transpose(ps_side[:, 3 * P:4 * P], wo_order[:], ident).then_inc(weights_turned, 1)
            turn_group(0)
            pe.wait_ge(weights_ready, 1)

            def score_rows(it, k, s):
                ka, u = k + 1 + (s + LEAD) // 8, (s + LEAD) % 8
                if not exists(it, ka):
                    return
                done, buf = batch(it, ka) * 8 + u, ka % UNROLL
                t, half = u // 2, u % 2
                if u == 0:
                    pe.wait_ge(stack_loaded[buf], (it + ka // 4 + 1) * 80)
                if isinstance(it, int) and batch(it, ka) == 0 and u == 1:
                    pe.wait_ge(group_copied, GROUPS - 1)
                if due(count := done - 1):
                    pe.wait_ge(rows_reduced, count)
                for a in range(2):
                    ins = mm(ps_rows[u % 2][:, 2 * a:2 * a + 2, :], q_stack[:, buf, t, half * P:(half + 1) * P],
                             k_stack[:, buf, 4 * t + 2 * a:4 * t + 2 * a + 2, :], start=True, stop=True)
                ins.then_inc(rows_scored, 1)

            def score_cols(it, k, s):
                if not exists(it, k):
                    return
                buf = k % UNROLL
                if s % 2 == 0:
                    pe.wait_ge(shift_loaded[s // 2][k % 2], (it * 2 + k // 2 + 1) * 16)
                for h in (2 * s, 2 * s + 1):
                    done = batch(it, k) * HEADS + h
                    if due(count := done - 1):
                        pe.wait_ge(probs_ready, count)
                    for kt in range(2):
                        ins = mm(ps_cols[h % 2][:, kt * SEQ:(kt + 1) * SEQ], k_stack[:, buf, h, kt * P:(kt + 1) * P],
                                 q_stack[:, buf, h // 4, :], start=True, stop=True)
                    ins.then_inc(cols_scored, 1)

            def sum_values(it, k, s):
                k, s = (k, s - 2) if s >= 2 else (k - 1, s + 6)
                if not exists(it, k):
                    return
                buf, t, kt = k % UNROLL, s // 2, s % 2
                g, e = t // 2, t % 2
                if kt == 0:
                    pe.wait_ge(probs_ready, batch(it, k) * HEADS + 4 * t + 4)
                if s == 0:
                    if due(count := batch(it, k)):
                        pe.wait_ge(values_copied, count)
                    pe.wait_ge(side_read, side("v", it, k - k % 2))
                for j in range(4):
                    h = 4 * t + j
                    ins = mm(ps_values[32 * j:32 * j + 32, g * SEQ:(g + 1) * SEQ], v_pad[:, buf, kt, h, :],
                             probs[:, h % 8, kt * SEQ:(kt + 1) * SEQ],
                             start=(e == 0 and kt == 0), stop=(e == 1 and kt == 1))
                if kt == 1:
                    ins.then_inc(values_summed, 1)

            def side_job(it, k, s):
                name, ahead = job(it, k, s)
                j = k + ahead
                if name is None or not exists(it, j):
                    return
                if due(count := side(name, it, j) - 1):
                    pe.wait_ge(side_read, count)
                r = (j // 2) % 2
                if name in ("q", "k"):
                    w = (wqT, wkT)[int(name == "k")]
                    pe.wait_ge(xc_loaded[r], (it + j // 4 + 1) * 16)
                    for two in range(2):
                        for b in range(2):
                            ins = mm(ps_side[b * P // 2:(b + 1) * P // 2, two * SEQ:(two + 1) * SEQ],
                                     w[:, two * P // 2:(two + 1) * P // 2], xc[:, r, b * SEQ:(b + 1) * SEQ],
                                     start=True, stop=True)
                elif name == "v":
                    pe.wait_ge(xc_loaded[r], (it + j // 4 + 1) * 16)
                    for i in range(4):
                        ins = mm(ps_side[:, i * P:(i + 1) * P], xc[:, r, i * P:(i + 1) * P], wvT[:],
                                 start=True, stop=True)
                elif name == "turn_maxima":
                    pe.wait_ge(rows_reduced, batch(it, j) * 8 + 8)
                    for half in range(2):
                        ins = nc.tensor.transpose(ps_side16[0:HEADS, half * P:(half + 1) * P],
                                                  maxima[:, j % 2, half, :], ident16[:])
                elif name == "turn_values":
                    pe.wait_ge(values_copied, batch(it, j) + 1)
                    for g in range(2):
                        for half in range(2):
                            to = (2 * half + g) * P
                            ins = nc.tensor.transpose(ps_side[:, to:to + P],
                                                      valuesT[:, g * SEQ + half * P:g * SEQ + (half + 1) * P], ident)
                elif name == "weight8":
                    pe.wait_ge(weight_step, 10)
                    nc.tensor.transpose(ps_sideb[:, 0:P], w8[:], identb[:])
                    pe.wait_ge(wide_ready, 1)
                    ins = mm(ps_side[:, P:2 * P], bv_wide[:], woT[:], start=True, stop=True)
                elif name == "turn_heads":
                    pe.wait_ge(side_read, side("turn_values", it, j))
                    for half in range(2):
                        ins = nc.tensor.transpose(ps_side[:, half * P:(half + 1) * P],
                                                  heads[:, half * P:(half + 1) * P], ident)
                else:
                    pe.wait_ge(side_read, side("turn_heads", it, j))
                    pe.wait_ge(x8_ready, batch(it, j) + 1)
                    for half in range(2):
                        mm(ps_side[:, half * P:(half + 1) * P], headsT[:, half * P:(half + 1) * P], woT[:],
                           start=True, stop=True)
                    for half in range(2):
                        ins = mm(ps_side[:, SEQ + half * P:SEQ + (half + 1) * P],
                                 x8[:, j % 2, half * P:(half + 1) * P], w8T[:], start=True, stop=True)
                ins.then_inc(side_written, 1)

            def pe_batch(it, k):
                for s in range(8):
                    score_rows(it, k, s)
                    score_cols(it, k, s)
                    sum_values(it, k, s)
                    side_job(it, k, s)
                    if group := group_at(TURN_GROUPS, it, k, s):
                        turn_group(group)

            def body(it):
                for k in range(UNROLL):
                    pe_batch(it, k)

            rounds(pe, body)
            pe_batch(ROUNDS, 0)
            pe_batch(ROUNDS, 1)


_INS = ["L0_attn_x", "L0_attn_Wq", "L0_attn_bq", "L0_attn_Wk", "L0_attn_bk", "L0_attn_Wv", "L0_attn_bv",
        "L0_attn_Wo", "L0_attn_bo", "L0_ffn_weight", "L0_ffn_bias"]


def constant_tables():
    import numpy as np

    half = P // 2
    steps = np.arange(half, dtype=np.float32) / np.float32(half)
    frequency = np.float32(1.0) / np.power(np.float32(10000.0), steps, dtype=np.float32)
    angle = np.arange(SEQ, dtype=np.float32)[None, :] * frequency[:, None]
    t = np.zeros((P, T_COLS), np.float32)
    t[:, T_ID:T_ID + P] = np.eye(P, dtype=np.float32)
    t[:, T_COS:T_COS + SEQ] = np.tile(np.cos(angle, dtype=np.float32), (2, 1))
    t[:, T_SIN:T_SIN + 2 * SEQ] = np.tile(np.sin(angle, dtype=np.float32), (2, 2))
    t[:, T_SIN:T_SIN + SEQ] *= np.float32(-1.0)
    t[0::HEAD // 2, T_FLAG] = 1.0
    return t


def kernel(**inputs):
    import numpy as np
    from concourse import bacc
    from concourse.bass_utils import run_bass_kernel_spmd

    nc = bacc.Bacc("TRN2", target_bir_lowering=False, num_devices=1)
    arrays = {"tables": constant_tables()}
    args = [nc.dram_tensor("tables", (P, T_COLS), F32, kind="ExternalInput").ap()]
    for name in _INS:
        a = np.ascontiguousarray(inputs[name])
        arrays[f"in_{name}"] = a
        args.append(nc.dram_tensor(f"in_{name}", a.shape, mybir.dt.from_np(a.dtype), kind="ExternalInput").ap())
    out = nc.dram_tensor("out", (BATCH, SEQ, P), F32, kind="ExternalOutput").ap()
    attention_and_ffn(nc, *args, out)
    r = run_bass_kernel_spmd(nc, [arrays], core_ids=[0])
    return r.results[0]["out"]
```
